# Optimizing a Trainium2 kernel written in Bass

```python
import numpy as np
import jax
import jax.numpy as jnp

def _softmax(x, axis=-1):
    return jax.nn.softmax(x, axis=axis)

def _gelu(x):
    return jax.nn.gelu(x, approximate=True)

def _silu(x):
    return jax.nn.silu(x)

def _sigmoid(x):
    return jax.nn.sigmoid(x)

def _layernorm(x, axis=-1, eps=1e-05):
    m = jnp.mean(x, axis=axis, keepdims=True)
    v = jnp.var(x, axis=axis, keepdims=True)
    return (x - m) / jnp.sqrt(v + eps)

def _scatter_add(tgt, idx, src, axis=0):
    return tgt.at[idx].add(src)

def _segment_sum(src, seg, n):
    return jax.ops.segment_sum(src, seg, n)
kernel_name = 'mk_adaln_d1_jaxref_r4_6c6e47'

def setup_inputs(seed: int=0):
    np.random.seed(seed)
    _w = jnp.asarray

    def _L0_attn_setup():
        import jax, jax.numpy as jnp
        import numpy as np
        D_MODEL = 256
        N_HEADS = 16
        HEAD_DIM = D_MODEL // N_HEADS
        NEG_INF = jnp.float32(-1e+30)

        def _alibi_causal_mask(S, dtype):
            q = jnp.arange(S)[:, None]
            k = jnp.arange(S)[None, :]
            return jnp.where(k <= q, -(q - k).astype(dtype), NEG_INF)
        key = jax.random.key(seed)
        ks = jax.random.split(key, 5)
        B, S, D = (4, 512, D_MODEL)
        scale = 1.0 / np.sqrt(D)
        x = jax.random.normal(ks[0], (B, S, D), dtype=jnp.float32)
        w_qkv = jax.random.normal(ks[1], (3 * D, D), dtype=jnp.float32) * scale
        b_qkv = jnp.zeros((3 * D,), dtype=jnp.float32)
        w_out = jax.random.normal(ks[2], (D, D), dtype=jnp.float32) * scale
        b_out = jnp.zeros((D,), dtype=jnp.float32)
        return {'x': x, 'w_qkv': w_qkv, 'b_qkv': b_qkv, 'w_out': w_out, 'b_out': b_out}
    _L0_attn_in = _L0_attn_setup()

    def _L0_ffn_setup():
        import jax, jax.numpy as jnp
        import numpy as np
        TOP_P = 0.3
        key = jax.random.key(seed)
        k1, k2, k3, k4 = jax.random.split(key, 4)
        B, S, D, H, E = (4, 1024, 256, 256, 8)
        x = jax.random.normal(k1, (B, S, D), dtype=jnp.float32)
        gate_W = jax.random.normal(k2, (E, D), dtype=jnp.float32) / np.float32(np.sqrt(D))
        expert_W = jax.random.normal(k3, (E, H, D), dtype=jnp.float32) / np.float32(np.sqrt(D))
        out_W = jax.random.normal(k4, (D, H), dtype=jnp.float32) / np.float32(np.sqrt(H))
        return {'x': x, 'gate_W': gate_W, 'expert_W': expert_W, 'out_W': out_W}
    _L0_ffn_in = _L0_ffn_setup()
    _L0_c = _w((lambda *s: np.random.randn(*s).astype(np.float32) * 0.05)(32, 256))
    _L0_wmod = _w((lambda *s: np.random.randn(*s).astype(np.float32) * 0.05)(256, 6 * 256) * 256 ** (-0.5))
    _d = {'L0_attn_x': _L0_attn_in['x'], 'L0_attn_w_qkv': _L0_attn_in['w_qkv'], 'L0_attn_b_qkv': _L0_attn_in['b_qkv'], 'L0_attn_w_out': _L0_attn_in['w_out'], 'L0_attn_b_out': _L0_attn_in['b_out'], 'L0_ffn_gate_W': _L0_ffn_in['gate_W'], 'L0_ffn_expert_W': _L0_ffn_in['expert_W'], 'L0_ffn_out_W': _L0_ffn_in['out_W'], 'L0_c': _L0_c, 'L0_wmod': _L0_wmod}
    _x0 = _d['L0_attn_x']
    _d['L0_attn_x'] = jax.random.normal(jax.random.fold_in(jax.random.key(seed), 1), (32, 512, 256), dtype=_x0.dtype)
    del _x0
    return _d

def reference(L0_attn_x, L0_attn_w_qkv, L0_attn_b_qkv, L0_attn_w_out, L0_attn_b_out, L0_ffn_gate_W, L0_ffn_expert_W, L0_ffn_out_W, L0_c, L0_wmod):

    def _L0_attn_ref(x, w_qkv, b_qkv, w_out, b_out):
        import jax, jax.numpy as jnp
        import numpy as np
        D_MODEL = 256
        N_HEADS = 16
        HEAD_DIM = D_MODEL // N_HEADS
        NEG_INF = jnp.float32(-1e+30)

        def _alibi_causal_mask(S, dtype):
            q = jnp.arange(S)[:, None]
            k = jnp.arange(S)[None, :]
            return jnp.where(k <= q, -(q - k).astype(dtype), NEG_INF)
        B, S, D = x.shape
        H, hd = (N_HEADS, HEAD_DIM)
        qkv = x @ w_qkv.T + b_qkv
        q, k, v = jnp.split(qkv, 3, axis=-1)
        q = q.reshape(B, S, H, hd).transpose(0, 2, 1, 3)
        k = k.reshape(B, S, H, hd).transpose(0, 2, 1, 3)
        v = v.reshape(B, S, H, hd).transpose(0, 2, 1, 3)
        scores = jnp.einsum('bhqd,bhkd->bhqk', q, k) / np.sqrt(hd)
        scores = scores + _alibi_causal_mask(S, scores.dtype)
        probs = jax.nn.softmax(scores, axis=-1)
        out = jnp.einsum('bhqk,bhkd->bhqd', probs, v)
        out = out.transpose(0, 2, 1, 3).reshape(B, S, D)
        return out @ w_out.T + b_out

    def _L0_ffn_ref(x, gate_W, expert_W, out_W):
        import jax, jax.numpy as jnp
        import numpy as np
        TOP_P = 0.3
        B, S, D = x.shape
        E = gate_W.shape[0]
        N = B * S
        p = jax.nn.softmax(jnp.einsum('bsd,ed->bse', x, gate_W), axis=-1).reshape(N, E)
        tpi = (p > TOP_P).astype(jnp.int32)
        cnt = jnp.sum(tpi[:, :, None] == jnp.arange(E)[None, None, :], axis=1)
        scale = cnt.astype(x.dtype) * p
        x2 = x.reshape(N, D)
        h = jnp.einsum('nd,ehd->neh', x2, expert_W)
        final = jnp.einsum('neh,ne->nh', h, scale)
        out = jnp.einsum('nh,dh->nd', final, out_W).reshape(B, S, D)
        return out
    x = L0_attn_x
    mod = (_silu(L0_c) @ L0_wmod).reshape(L0_c.shape[0], 6, 1, -1)
    sa, ca, ga, sb, cb, gb = (mod[:, 0], mod[:, 1], mod[:, 2], mod[:, 3], mod[:, 4], mod[:, 5])
    ga = (2 * (ga >= 0) - 1) * jnp.maximum(jnp.abs(ga), 0.25)
    gb = (2 * (gb >= 0) - 1) * jnp.maximum(jnp.abs(gb), 0.25)
    h = _layernorm(x, axis=-1) * (1 + ca) + sa
    x = x + ga * _L0_attn_ref(h, L0_attn_w_qkv, L0_attn_b_qkv, L0_attn_w_out, L0_attn_b_out)
    h = _layernorm(x, axis=-1) * (1 + cb) + sb
    x = x + gb * _L0_ffn_ref(h, L0_ffn_gate_W, L0_ffn_expert_W, L0_ffn_out_W)
    return x

_drawn_inputs = setup_inputs


def setup_inputs(seed=0):
    import zlib

    import numpy as np

    out = dict(_drawn_inputs(seed))
    spreads = {'L0_attn_b_qkv': (0.0, 0.294), 'L0_attn_b_out': (0.0, 0.32)}
    factors = {}
    for name, (base, spread) in spreads.items():
        noise = np.random.default_rng([zlib.crc32(name.encode()), seed]).standard_normal(out[name].shape)
        drawn = base * np.exp(spread * noise) if base else spread * noise
        out[name] = jnp.asarray(drawn.astype(out[name].dtype))
    for name, factor in factors.items():
        out[name] = (out[name] * factor).astype(out[name].dtype)
    return out
```

```python
from contextlib import ExitStack

import numpy as np

import concourse.bass as bass
from concourse import mybir

F32 = mybir.dt.float32
F16 = mybir.dt.float16
BF16 = mybir.dt.bfloat16
ALU = mybir.AluOpType
ACT = mybir.ActivationFunctionType
AX = mybir.AxisListType

P = 128
WS = 16.0
FS = 4 * WS * WS
QONE = 64.0
EPS = 1e-5
TOP_P = 0.3
SLOTS = 16
LOADS = 14
TURNED_AT, ROWS_AT, SET_DVE = 18, 26, 34
SET_PE = 2
STACK_DMAS = 10


def build(nc, x, w_qkv, b_qkv, w_out, b_out, gate_w, expert_w, out_w, cond, wmod,
          ident_d, mask_kq_d, mask_qk_d, kaug_d, out):
    NB, S, D = x.shape
    H, HD = 16, 16
    QT = S // P
    DC = D // P
    E = gate_w.shape[0]
    HP = H // 2
    assert (S, D, QT, DC) == (512, 256, 4, 2) and E == 8

    ctx = ExitStack()
    with ctx:
        def sb(name, shape, dt):
            return ctx.enter_context(nc.sbuf_tensor(name, shape, dt))

        def sem(name):
            return ctx.enter_context(nc.semaphore(name))

        def dram(name, shape, dt):
            return nc.dram_tensor(name, shape, dt, kind="Internal").ap()

        ps = ctx.enter_context(nc.psum_tensor("ps", [P, 8, 512], F32))
        ST, MX, PVB, MISC = 0, 3, 5, 6

        ident = sb("ident", [P, P], F32)
        identb = sb("identb", [P, P], BF16)
        mask_kq = sb("mask_kq", [P, P], BF16)
        mask_qk = sb("mask_qk", [P, P], BF16)
        wqkv_hi = sb("wqkv_hi", [P, DC, 3 * D], F16)
        wqkv_lo = sb("wqkv_lo", [P, DC, 3 * D], F16)
        wo_hi = sb("wo_hi", [P, DC, D], F16)
        wo_lo = sb("wo_lo", [P, DC, D], F16)
        moe_hi = sb("moe_hi", [P, DC, 2 * D], F16)
        moe_lo = sb("moe_lo", [P, DC, 2 * D], F16)
        gw_hi = sb("gw_hi", [P, DC, E], F16)
        gw_lo = sb("gw_lo", [P, DC, E], F16)
        bqk = sb("bqk", [P, 4], F32)
        bv = sb("bv", [P, DC], F32)
        modT = sb("modT", [P, NB, 8], F32)
        zrow = sb("zrow", [2, 4 * S], F16)

        qs = sb("qs", [P, HP, S], F16)
        kz = sb("kz", [P, H, S], F16)
        prob = sb("prob", [P, 8, 10 * P], F32)
        va = sb("va", [P, QT, H, 32], F32)
        vst = sb("vst", [P, QT, D], F32)
        mxt = sb("mxt", [P, 4, 16], F32)
        negm = sb("negm", [16, P], F16)
        xa = sb("xa", [P, QT, D], F32)
        xn_a = sb("xn_a", [P, QT, D], F32)
        mod_a = sb("mod_a", [P, 4], F32)
        st_a = sb("st_a", [P, QT, 6], F32)
        mv_a = sb("mv_a", [P, QT, 2], F32)
        ve_a = sb("ve_a", [P, QT], F32)
        nm_a = sb("nm_a", [P, QT], F32)
        rs_a = sb("rs_a", [P, QT], F32)
        hf_a = sb("hf_a", [P, DC, S], F32)
        hh_a = sb("hh_a", [P, DC, S], F16)
        hl_a = sb("hl_a", [P, DC, S], F16)
        qk_st = sb("qk_st", [P, 2, 2, S], F16)
        ou = sb("ou", [P, 4, S], F32)
        oc = sb("oc", [P, DC, S], F32)
        zc = sb("zc", [64, P], F32)
        zr = sb("zr", [64, P], F32)
        rz = sb("rz", [P, DC, S], F32)
        om = sb("om", [P, DC, S], F32)
        oh = sb("oh", [P, DC, S], F16)
        ol = sb("ol", [P, DC, S], F16)
        xc = sb("xc", [P, QT, D], F32)
        xg = sb("xg", [P, QT, D], F32)
        ga_bc = sb("ga_bc", [P, 2, D], F32)
        gb_bc = sb("gb_bc", [P, D], F32)
        ot = sb("ot", [P, QT, D], F32)
        x1 = sb("x1", [P, QT, D], F32)
        xn_c = sb("xn_c", [P, QT, D], F32)
        mod_c = sb("mod_c", [P, 4], F32)
        st_c = sb("st_c", [P, QT, 6], F32)
        mv_c = sb("mv_c", [P, QT, 2], F32)
        ve_c = sb("ve_c", [P, QT], F32)
        nm_c = sb("nm_c", [P, QT], F32)
        rs_c = sb("rs_c", [P, QT], F32)
        hf_c = sb("hf_c", [P, DC, S], F32)
        hh_c = sb("hh_c", [P, DC, S], F16)
        hl_c = sb("hl_c", [P, DC, S], F16)
        gmax = sb("gmax", [P, QT], F32)
        gsub = sb("gsub", [P, QT, E], F32)
        gexp = sb("gexp", [P, QT, E], F32)
        gsum = sb("gsum", [P, QT], F32)
        grec = sb("grec", [P, QT], F32)
        gp = sb("gp", [P, QT, E], F32)
        gtop = sb("gtop", [P, QT, E], F32)
        gcnt = sb("gcnt", [P, QT], F32)
        gcnt0 = sb("gcnt0", [P, QT], F32)
        scl = sb("scl", [P, 2, QT], F32)
        z0 = sb("z0", [P, QT, D], F32)
        zs = sb("zs", [P, QT, D], F32)
        zg = sb("zg", [P, QT, D], F32)
        res = sb("res", [P, QT, D], F32)
        neg_half = sb("neg_half", [P, QT], F32)

        spare = prob[:].rearrange("p a b -> p (a b)")
        taken = [0]

        def lend(rows, *dims):
            size = int(np.prod(dims))
            got = spare[0:rows, taken[0]:taken[0] + size]
            taken[0] += size
            if len(dims) == 2:
                got = got.rearrange("p (a b) -> p a b", a=dims[0])
            if len(dims) == 3:
                got = got.rearrange("p (a b c) -> p a b c", a=dims[0], b=dims[1])
            return got

        wq_nat, wo_nat, ow_nat = lend(P, 6, D), lend(P, DC, D), lend(P, DC, D)
        ex_nat, g_nat, c_nat = lend(P, 2, DC, D), lend(E, D), lend(NB, D)
        wm_nat, b_raw, bo_bc = lend(P, DC, 6 * D), lend(P, 4), lend(NB, D)
        c_exp, c_silu, c_silu_t = lend(NB, D), lend(NB, D), lend(P, DC, NB)
        g_sgn, g_abs, mrow = lend(NB, 2 * D), lend(NB, 2 * D), lend(NB, 3 * D)
        m_nat = lend(P, 2, P)
        ow_t = vst[:, 0:2, :]

        qk_d = dram("qk_d", [2, 2, 2, P, S], F16)
        negm_d = dram("negm_d", [4, 16, P], F16)
        ou_d = dram("ou_d", [4 * P, S], F32)
        rz_d = dram("rz_d", [H, S], F32)
        rows_d = dram("rows_d", [NB, 3 * D], F32)

        block = ctx.enter_context(nc.Block())
        s = {}

        def sm(name):
            if name not in s:
                s[name] = sem(name)
            return s[name]

        for name in ("ld_w", "set_dve", "set_pe", "set_act", "set_ready", "rows_stored", "kaug_loaded",
                     "xa_loaded", "moda_loaded", "lna_stats", "lna_aggr", "lna_ready", "rsa_ready", "xna_ready",
                     "ta_ready", "hfa_ready", "hha_ready", "hla_ready", "qk_ready", "qk_hi", "qk_lo",
                     "qk_stored0", "qk_stored1", "qk_stored2", "qk_stored3", "stack_loaded0", "stack_loaded1",
                     "v_ready", "v_evicted", "va_ready", "mx_ready", "mx_read", "mt_ready", "nm_ready",
                     "nm_stored", "aug_loaded", "st_ready", "exp_done", "pv_done", "ou_ready", "ou_stored",
                     "zc_loaded", "oc_loaded", "zr_ready", "rz_stored", "rz_loaded", "om_ready", "oh_ready",
                     "ol_ready", "out_ready", "ot_ready", "x1_ready", "xc_loaded", "ga_loaded", "xg_ready",
                     "lnc_stats", "lnc_aggr", "lnc_ready", "rsc_ready", "xnc_ready", "modc_loaded", "gb_loaded",
                     "t2_ready", "hfc_ready", "hhc_ready", "hlc_ready", "gate_ready", "gate_step", "gate_exp",
                     "scl_ready", "moe_ready", "z0_ready", "zs_ready", "zg_ready", "res_ready", "res_stored",
                     "passed_sp", "passed_dve", "passed_pool"):
            sm(name)

        def wait(eng, name, value, passed=None):
            if isinstance(value, int) and value <= 0:
                return
            eng.wait_ge(s[name], value)
            if passed and not isinstance(value, int):
                eng.sem_inc(s[passed], 1)

        SIDE = {
            0: [("ta", 0, 1, 0), ("ta", 1, 1, 1)],
            2: [("qk", 0, 1, 0), ("mt", 1, 0, 1)],
            3: [("t2", 0, -2, 0), ("t2", 1, -2, 1)],
            4: [("qk", 1, 1, 0)],
            5: [("gate", 0, -2, 1)],
            6: [("moe", 0, -2, 0), ("mt", 2, 0, 1)],
            7: [("moe", 1, -2, 0)],
            8: [("qk", 2, 1, 1)],
            9: [("qk", 3, 1, 0)],
            10: [("moe", 2, -2, 1), ("mt", 3, 0, 0)],
            11: [("moe", 3, -2, 1)],
            12: [("v", 0, 1, 0)],
            13: [("v", 1, 1, 1)],
            14: [("out", 0, -1, 0), ("mt", 0, 1, 1)],
            15: [("out", 1, -1, 0)],
        }
        READ = {"ta": ("hha_ready", 2), "qk": ("qk_lo", 4), "mt": ("nm_ready", 4), "t2": ("hhc_ready", 2),
                "gate": ("gate_step", 8), "moe": ("zs_ready", 4), "v": ("v_evicted", 2), "out": ("ot_ready", 2)}

        def live(b):
            return not isinstance(b, int) or 0 <= b < NB

        def iterations(eng, one, first=-2):
            for i in range(first, 2):
                one(i)
            with eng.Fori(2, NB - 2) as i:
                one(i)
            for i in range(NB - 2, NB + 2):
                one(i)

        def side(i, t):
            for name, n, off, bank in SIDE.get(t, []):
                if live(i + off):
                    yield name, n, i + off, bank

        def before(i, t, pos, bank):
            order = [(u, q, st) for u in sorted(SIDE) for q, st in enumerate(SIDE[u])]
            at = [n for n, (u, q, _) in enumerate(order) if (u, q) == (t, pos)][0]
            for back in range(1, 3 * len(order)):
                laps, n = divmod(at - back, len(order))
                name, idx, off, bk = order[n][2]
                if bk == bank and live(i + off + laps):
                    return name, idx, i + off + laps
                if bk == bank and isinstance(i, int) and i + off + laps < 0 and laps < -1:
                    return None
            return None

        def max_at(i, t):
            return (i + 1, t - 10) if t >= 10 else (i, t + 6)

        PCOL = [0, 512, 1024, 896]
        CHUNK = [(0, 512, [0]), (512, 512, [1, 3]), (1024, 256, [2])]
        MPART = [[3], [2, 0], [1]]

        @block.sync
        def _(sp):
            n = [0]

            def ld(dst, src, **kw):
                sp.dma_start(dst, src, **kw).then_inc(s["ld_w"], 16)
                n[0] += 1
            ld(ident[:], ident_d)
            ld(wq_nat, w_qkv.rearrange("(k p) d -> p k d", p=P))
            ld(wo_nat, w_out.rearrange("(k p) d -> p k d", p=P))
            ld(ow_nat, out_w.rearrange("(k p) d -> p k d", p=P))
            for e in range(2):
                ld(ex_nat[:, e], expert_w[e].rearrange("(k p) d -> p k d", p=P))
            ld(g_nat, gate_w)
            ld(c_nat, cond)
            ld(wm_nat, wmod.rearrange("(k p) n -> p k n", p=P))
            ld(m_nat[:, 0], mask_kq_d)
            ld(m_nat[:, 1], mask_qk_d)
            ld(b_raw, b_qkv[0:2 * D].rearrange("(c p) -> p c", p=P), allow_slow_non_contiguous=True)
            ld(bv[:], b_qkv[2 * D:3 * D].rearrange("(c p) -> p c", p=P), allow_slow_non_contiguous=True)
            ld(bo_bc, b_out.rearrange("(o d) -> o d", o=1).broadcast_to([NB, D]))
            assert n[0] == LOADS, n[0]
            sp.wait_ge(s["set_ready"], 3)
            sp.dma_start(kz[0:3, :, :], kaug_d).then_inc(s["kaug_loaded"], 16)
            wait(sp, "set_dve", ROWS_AT, "passed_sp")
            sp.dma_start(rows_d, mrow).then_inc(s["rows_stored"], 16)
            sp.wait_ge(s["rows_stored"], 16)
            sp.wait_ge(s["kaug_loaded"], 16)
            wait(sp, "set_dve", SET_DVE, "passed_sp")
            wait(sp, "set_pe", SET_PE, "passed_sp")
            wait(sp, "set_ready", 3, "passed_sp")

            def load_a(b):
                wait(sp, "xna_ready", b * QT, "passed_sp")
                sp.dma_start(xa[:], x[b].rearrange("(t p) d -> p t d", p=P)).then_inc(s["xa_loaded"], 16)
                wait(sp, "hha_ready", b * 2, "passed_sp")
                sp.dma_start(mod_a[:], modT[:, b, 0:4]).then_inc(s["moda_loaded"], 16)

            def store_qk(b, n):
                wait(sp, "qk_lo", b * 4 + n + 1, "passed_sp")
                wait(sp, f"stack_loaded{n // 2}", b * STACK_DMAS * 16, "passed_sp")
                sp.dma_start(qk_d[n % 2, n // 2].rearrange("l p t -> p l t"), qk_st[:, n % 2]).then_inc(
                    s[f"qk_stored{n}"], 16)

            def load_stack(b, c):
                wait(sp, f"qk_stored{2 * c}", (b + 1) * 16, "passed_sp")
                wait(sp, f"qk_stored{2 * c + 1}", (b + 1) * 16, "passed_sp")
                wait(sp, "st_ready", b * 48 - 48 + 24 * (c + 1), "passed_sp")
                done = s[f"stack_loaded{c}"]
                pr = slice(4 * c, 4 * c + 4)
                sp.dma_start(qs[1:3, pr, :], zrow[:].rearrange("p (a t) -> p a t", a=4)).then_inc(done, 16)
                for r, part in enumerate((0, 0, 1)):
                    sp.dma_start(qs[32 * (r + 1):32 * (r + 2), pr, :],
                                 qk_d[0, c, part].rearrange("(a r) t -> r a t", a=4)).then_inc(done, 16)
                for r, part in enumerate((0, 1, 0)):
                    for j in range(2):
                        lo = 32 * (r + 1) + 16 * j
                        sp.dma_start(kz[lo:lo + 16, 8 * c + j:8 * c + 8:2, :],
                                     qk_d[1, c, part].rearrange("(a j r) t -> j r a t", a=4, j=2)[j]
                                     ).then_inc(done, 16)

            def store_negm(b, g):
                wait(sp, "nm_ready", b * 4 + g + 1, "passed_sp")
                wait(sp, "aug_loaded", (b * 4 + g) * 16, "passed_sp")
                sp.dma_start(negm_d[g], negm[:]).then_inc(s["nm_stored"], 16)

            def load_aug(b, g):
                wait(sp, "nm_stored", (b * 4 + g + 1) * 16, "passed_sp")
                sp.dma_start(qs[1:3, 2 * g:2 * g + 2, :],
                             negm_d[g].rearrange("(a j t) c -> j a (t c)", a=2, j=2)).then_inc(s["aug_loaded"], 16)

            def store_ou(b, g):
                wait(sp, "ou_ready", b * 4 + g + 1, "passed_sp")
                wait(sp, "oc_loaded", b * 32, "passed_sp")
                wait(sp, "zc_loaded", b * 16, "passed_sp")
                sp.dma_start(ou_d[P * g:P * (g + 1), :], ou[:, g, :]).then_inc(s["ou_stored"], 16)

            def load_o(b):
                wait(sp, "ou_stored", (b + 1) * 64, "passed_sp")
                wait(sp, "zr_ready", b, "passed_sp")
                sp.dma_start(zc[:], ou_d.rearrange("(h r) (u t) -> h r u t", r=32, u=4)[:, 16]).then_inc(
                    s["zc_loaded"], 16)
                wait(sp, "om_ready", b, "passed_sp")
                for c in range(DC):
                    src = ou_d.rearrange("(c h r) t -> c h r t", c=DC, r=32)[c, :, 0:HD, :]
                    sp.dma_start(oc[:, c, :], src).then_inc(s["oc_loaded"], 16)

            def store_rz(b):
                wait(sp, "zr_ready", b + 1, "passed_sp")
                wait(sp, "rz_loaded", b * 32, "passed_sp")
                sp.dma_start(rz_d.rearrange("h (u t) -> (h u) t", u=4), zr[:]).then_inc(s["rz_stored"], 16)

            def load_rz(b):
                wait(sp, "rz_stored", (b + 1) * 16, "passed_sp")
                for c in range(DC):
                    src = rz_d[8 * c:8 * c + 8, :].rearrange("h (o t) -> h o t", o=1).broadcast_to([8, HD, S])
                    sp.dma_start(rz[:, c, :], src).then_inc(s["rz_loaded"], 16)

            def load_c(b):
                wait(sp, "xg_ready", b, "passed_sp")
                sp.dma_start(xc[:], x[b].rearrange("(t p) d -> p t d", p=P)).then_inc(s["xc_loaded"], 16)

            def load_ga(b):
                wait(sp, "ot_ready", b * 2, "passed_sp")
                src = rows_d[bass.ds(b, 1), 0:2 * D].rearrange("o (k d) -> o k d", k=2).broadcast_to([P, 2, D])
                sp.dma_start(ga_bc[:], src).then_inc(s["ga_loaded"], 16)

            def load_gb(b):
                wait(sp, "zg_ready", b * 2, "passed_sp")
                sp.dma_start(gb_bc[:], rows_d[bass.ds(b, 1), 2 * D:3 * D].broadcast_to([P, D])).then_inc(
                    s["gb_loaded"], 16)

            def load_modc(b):
                wait(sp, "hhc_ready", b * 2, "passed_sp")
                sp.dma_start(mod_c[:], modT[:, b, 4:8]).then_inc(s["modc_loaded"], 16)

            def store_res(b):
                wait(sp, "res_ready", (b + 1) * 2, "passed_sp")
                sp.dma_start(out[b].rearrange("(t p) d -> p t d", p=P), res[:]).then_inc(s["res_stored"], 16)

            SP = {
                0: [(load_stack, 1, 0)],
                1: [(load_gb, None, -2)],
                2: [(load_c, None, -1), (store_negm, 1, 0)],
                3: [(load_aug, 1, 0), (load_a, None, 2)],
                4: [(store_qk, 0, 1), (store_ou, 3, -1)],
                5: [(load_ga, None, -1), (load_o, None, -1), (store_qk, 1, 1)],
                6: [(store_negm, 2, 0)],
                7: [(load_aug, 2, 0), (store_rz, None, -1)],
                8: [(load_stack, 0, 1), (load_rz, None, -1), (store_ou, 0, 0)],
                10: [(store_qk, 2, 1), (store_negm, 3, 0)],
                11: [(load_aug, 3, 0), (store_qk, 3, 1)],
                12: [(store_ou, 1, 0), (load_modc, None, -1)],
                13: [(store_res, None, -2)],
                14: [(store_negm, 0, 1)],
                15: [(load_aug, 0, 1)],
            }
            SP[0].append((store_ou, 2, -1))

            def one(i):
                for t in range(SLOTS):
                    for f, n, off in SP.get(t, []):
                        if live(i + off):
                            f(*([i + off] if n is None else [i + off, n]))

            iterations(sp, one)
            wait(sp, "res_stored", NB * 16, "passed_sp")

        @block.tensor
        def _(pe):
            mm = nc.tensor.matmul

            pe.wait_ge(s["ld_w"], LOADS * 16)

            def turn(n, src, rows=P):
                return nc.tensor.transpose(ps[:, n // 4, (n % 4) * P:(n % 4) * P + rows], src, ident[0:rows, 0:rows])

            for c in range(DC):
                for k in range(6):
                    turn(c * 6 + k, wq_nat[:, k, c * P:(c + 1) * P])
                for k in range(DC):
                    turn(12 + c * 2 + k, wo_nat[:, k, c * P:(c + 1) * P])
                    turn(16 + c * 2 + k, ow_nat[:, k, c * P:(c + 1) * P])
            pe.wait_ge(s["set_act"], 1)
            pe.wait_ge(s["set_dve"], 4)
            for c in range(DC):
                turn(20 + c, g_nat[:, c * P:(c + 1) * P], E)
                x_ = turn(22 + c, c_silu[:, c * P:(c + 1) * P], NB)
            x_.then_inc(s["set_pe"], 1)
            pe.wait_ge(s["set_dve"], TURNED_AT)
            for c in range(DC):
                for e in range(2):
                    for k in range(DC):
                        mm(ps[:, 6 + c, e * D:(e + 1) * D], ex_nat[:, e, k, c * P:(c + 1) * P],
                           ow_t[:, k, :], start=(k == 0), stop=(k == DC - 1))
            for n, part in enumerate((1, 0, 4, 3)):
                for c in range(DC):
                    for k in range(DC):
                        col = part * D + c * P
                        mm(ps[:, 0, (2 * n + c) * NB:(2 * n + c + 1) * NB], wm_nat[:, k, col:col + P],
                           c_silu_t[:, k, :], start=(k == 0), stop=(k == DC - 1))
            for n, part in enumerate((2, 5)):
                for k in range(DC):
                    x_ = mm(ps[0:NB, 1, n * D:(n + 1) * D], c_silu_t[:, k, :],
                            wm_nat[:, k, part * D:(part + 1) * D], start=(k == 0), stop=(k == DC - 1))
            x_.then_inc(s["set_pe"], 1)
            pe.wait_ge(s["set_dve"], SET_DVE)
            pe.wait_ge(s["set_ready"], 3)
            pe.wait_ge(s["kaug_loaded"], 16)

            def products(dst, pairs, last_sem=None):
                for n, (a, b) in enumerate(pairs):
                    x_ = mm(dst, a, b, start=(n == 0), stop=(n == len(pairs) - 1))
                return x_

            def side_step(name, n, b, bank, prev):
                if prev is not None:
                    pname, pn, pb = prev
                    rd, per = READ[pname]
                    wait(pe, rd, pb * per + (2 if pname == "gate" else pn + 1))
                dst = ps[:, MISC + bank, :]
                if name == "ta":
                    wait(pe, "xna_ready", (b + 1) * QT)
                    for t in range(QT):
                        x_ = nc.tensor.transpose(dst[:, t * P:(t + 1) * P], xn_a[:, t, n * P:(n + 1) * P], ident[:])
                    x_.then_inc(s["ta_ready"], 1)
                elif name == "t2":
                    wait(pe, "xnc_ready", (b + 1) * QT)
                    for t in range(QT):
                        x_ = nc.tensor.transpose(dst[:, t * P:(t + 1) * P], xn_c[:, t, n * P:(n + 1) * P], ident[:])
                    x_.then_inc(s["t2_ready"], 1)
                elif name == "qk":
                    wait(pe, "hla_ready", (b + 1) * 2)
                    col = (n % 2) * D + (n // 2) * P
                    w = slice(col, col + P)
                    pairs = []
                    for c in range(DC):
                        pairs += [(wqkv_hi[:, c, w], hh_a[:, c, :]), (wqkv_hi[:, c, w], hl_a[:, c, :]),
                                  (wqkv_lo[:, c, w], hh_a[:, c, :])]
                    products(dst, pairs).then_inc(s["qk_ready"], 1)
                elif name == "v":
                    for u in range(2):
                        t = slice((2 * n + u) * P, (2 * n + u + 1) * P)
                        pairs = []
                        for c in range(DC):
                            pairs += [(hh_a[:, c, t], wqkv_hi[:, c, 2 * D:]), (hh_a[:, c, t], wqkv_lo[:, c, 2 * D:]),
                                      (hl_a[:, c, t], wqkv_hi[:, c, 2 * D:])]
                        x_ = products(dst[:, u * D:(u + 1) * D], pairs)
                    x_.then_inc(s["v_ready"], 1)
                elif name == "mt":
                    wait(pe, "mx_read", b * 48 + 12 * (n + 1))
                    nc.tensor.transpose(dst[0:16, 0:P], mxt[:, n, :], ident[:]).then_inc(s["mt_ready"], 1)
                elif name == "out":
                    wait(pe, "ol_ready", (b + 1) * 2)
                    for u in range(2):
                        t = slice((2 * n + u) * P, (2 * n + u + 1) * P)
                        pairs = []
                        for c in range(DC):
                            pairs += [(oh[:, c, t], wo_hi[:, c, :]), (oh[:, c, t], wo_lo[:, c, :]),
                                      (ol[:, c, t], wo_hi[:, c, :])]
                        x_ = products(dst[:, u * D:(u + 1) * D], pairs)
                    x_.then_inc(s["out_ready"], 1)
                elif name == "gate":
                    wait(pe, "hlc_ready", (b + 1) * 2)
                    for u in range(QT):
                        t = slice(u * P, (u + 1) * P)
                        pairs = []
                        for c in range(DC):
                            pairs += [(hh_c[:, c, t], gw_hi[:, c, :]), (hh_c[:, c, t], gw_lo[:, c, :]),
                                      (hl_c[:, c, t], gw_hi[:, c, :])]
                        x_ = products(dst[:, u * E:(u + 1) * E], pairs)
                    x_.then_inc(s["gate_ready"], 1)
                elif name == "moe":
                    t = slice(n * P, (n + 1) * P)
                    pairs = []
                    for c in range(DC):
                        pairs += [(hh_c[:, c, t], moe_hi[:, c, :]), (hh_c[:, c, t], moe_lo[:, c, :]),
                                  (hl_c[:, c, t], moe_hi[:, c, :])]
                    products(dst, pairs).then_inc(s["moe_ready"], 1)

            def scores(b, h, n):
                if h % 4 == 0 and n == 0:
                    wait(pe, "aug_loaded", (b * 4 + h // 4 + 1) * 16)
                wait(pe, "exp_done", b * 48 + 3 * h + n - 2)
                col = 0
                for kt in CHUNK[n][2]:
                    w = (QT - kt) * P
                    mm(ps[:, ST + n, col:col + w], kz[:, h, kt * P:(kt + 1) * P], qs[:, h // 2, kt * P:],
                       start=True, stop=False)
                    x_ = mm(ps[:, ST + n, col:col + P], identb[:], mask_kq[:], start=False, stop=True)
                    col += w
                x_.then_inc(s["st_ready"], 1)

            def row_scores(b, h, n):
                if h % 8 == 0 and n == 0:
                    wait(pe, f"stack_loaded{h // 8}", (b + 1) * STACK_DMAS * 16)
                wait(pe, "mx_read", b * 48 + 3 * h + n - 1)
                bank = MX + (3 * h + n) % 2
                col = 0
                for qt in MPART[n]:
                    w = (qt + 1) * P
                    mm(ps[:, bank, col:col + w], qs[:, h // 2, qt * P:(qt + 1) * P], kz[:, h, 0:w],
                       start=True, stop=False)
                    x_ = mm(ps[:, bank, col + w - P:col + w], identb[:], mask_qk[:], start=False, stop=True)
                    col += w
                x_.then_inc(s["mx_ready"], 1)

            def weigh(b, g, kt):
                if kt == 0:
                    wait(pe, "exp_done", b * 48 + 12 * (g + 1))
                    wait(pe, "va_ready", b * 4 + g + 1)
                    wait(pe, "ou_ready", b * 4 + g)
                for j in range(4):
                    h = 4 * g + j
                    w = (QT - kt) * P
                    x_ = mm(ps[32 * j:32 * j + 32, PVB, kt * P:S], va[:, kt, h, :],
                            prob[:, h % 8, PCOL[kt]:PCOL[kt] + w], start=(kt == 0), stop=(kt == QT - 1))
                x_.then_inc(s["pv_done"], 1)

            def one(i):
                for t in range(SLOTS):
                    here = live(i)
                    bm, hm = max_at(i, t)
                    if here:
                        scores(i, t, 0)
                        scores(i, t, 1)
                    if live(bm):
                        row_scores(bm, hm, 0)
                    if here:
                        scores(i, t, 2)
                    if live(bm):
                        row_scores(bm, hm, 1)
                    for pos, (name, n, off, bank) in enumerate(SIDE.get(t, [])):
                        if live(i + off):
                            side_step(name, n, i + off, bank, before(i, t, pos, bank))
                    bp = i if t >= 4 else i - 1
                    if live(bp):
                        weigh(bp, (t // 4 - 1) % 4, t % 4)
                    if live(bm):
                        row_scores(bm, hm, 2)

            iterations(pe, one)

        @block.scalar
        def _(act):
            act.wait_ge(s["ld_w"], LOADS * 16)
            nc.scalar.activation(c_exp, c_nat, ACT.Exp, scale=-1.0).then_inc(s["set_act"], 1)
            wait(act, "set_dve", SET_DVE)
            wait(act, "set_ready", 3)
            wait(act, "rows_stored", 16)

            def exp(b, h, n):
                if n == 0 and h % 4 == 0:
                    wait(act, "pv_done", b * 16 + h - 4)
                wait(act, "st_ready", b * 48 + 3 * h + n + 1)
                at, w, _ = CHUNK[n]
                nc.scalar.activation(prob[:, h % 8, at:at + w], ps[:, ST + n, 0:w], ACT.Exp,
                                     scale=1.0 / FS).then_inc(s["exp_done"], 1)

            def turned(b, n, bank, ready, mod, loaded, hf, hh, hf_sem, hh_sem, hl_sem, users):
                wait(act, ready, b * 2 + n + 1)
                wait(act, loaded, (b + 1) * 16)
                wait(act, hl_sem, b * 2)
                for name, per in users:
                    wait(act, name, b * per)
                src = ps[:, MISC + bank, :]
                nc.scalar.activation(hf[:, n, :], src, ACT.Identity, bias=mod[:, 2 + n:3 + n],
                                     scale=mod[:, n:n + 1]).then_inc(s[hf_sem], 1)
                nc.scalar.activation(hh[:, n, :], src, ACT.Identity, bias=mod[:, 2 + n:3 + n],
                                     scale=mod[:, n:n + 1]).then_inc(s[hh_sem], 1)

            def side_step(name, n, b, bank):
                src = ps[:, MISC + bank, :]
                if name == "ta":
                    turned(b, n, bank, "ta_ready", mod_a, "moda_loaded", hf_a, hh_a, "hfa_ready", "hha_ready",
                           "hla_ready", [("v_ready", 2), ("qk_ready", 4)])
                elif name == "t2":
                    turned(b, n, bank, "t2_ready", mod_c, "modc_loaded", hf_c, hh_c, "hfc_ready", "hhc_ready",
                           "hlc_ready", [("moe_ready", 4)])
                elif name == "qk":
                    wait(act, "qk_ready", b * 4 + n + 1)
                    k = n % 2
                    if n >= 2:
                        wait(act, f"qk_stored{n - 2}", (b + 1) * 16)
                    else:
                        wait(act, f"qk_stored{n + 2}", b * 16)
                    nc.scalar.activation(qk_st[:, k, 0, :], src, ACT.Identity,
                                         bias=bqk[:, 2 * k + n // 2:2 * k + n // 2 + 1]).then_inc(s["qk_hi"], 1)
                elif name == "v":
                    wait(act, "v_ready", b * 2 + n + 1)
                    wait(act, "va_ready", b * 4)
                    nc.scalar.activation(vst[:, 2 * n:2 * n + 2, :], src.rearrange("p (u d) -> p u d", u=2),
                                         ACT.Copy, scale=1.0 / WS).then_inc(s["v_evicted"], 1)
                elif name == "mt":
                    wait(act, "mt_ready", b * 4 + n + 1)
                    wait(act, "nm_stored", (b * 4 + n) * 16)
                    nc.scalar.activation(negm[:], ps[0:16, MISC + bank, 0:P], ACT.Copy,
                                         scale=-1.0 / FS).then_inc(s["nm_ready"], 1)
                elif name == "moe":
                    wait(act, "moe_ready", b * 4 + n + 1)
                    wait(act, "scl_ready", b + 1)
                    wait(act, "zs_ready", b * 4)
                    nc.scalar.activation(z0[:, n, :], ps[:, MISC + bank, 0:D], ACT.Copy,
                                         scale=scl[:, 0, n:n + 1]).then_inc(s["z0_ready"], 1)

            def sums_out(b, g):
                wait(act, "pv_done", b * 16 + 4 * g + 4)
                if g == 0:
                    wait(act, "ou_stored", b * 64)
                nc.scalar.activation(ou[:, g, :], ps[:, PVB, :], ACT.Copy).then_inc(s["ou_ready"], 1)

            def gate_exp(b):
                wait(act, "gate_step", b * 8 + 2)
                wait(act, "gate_step", b * 8)
                nc.scalar.activation(gexp[:], gsub[:], ACT.Exp, scale=1.0 / WS).then_inc(s["gate_exp"], 1)

            def o_hi(b):
                wait(act, "om_ready", b + 1)
                wait(act, "out_ready", b * 2)
                wait(act, "ol_ready", b * 2)
                for c in range(DC):
                    nc.scalar.activation(oh[:, c, :], om[:, c, :], ACT.Identity,
                                         bias=bv[:, c:c + 1]).then_inc(s["oh_ready"], 1)

            def one(i):
                for t in range(SLOTS):
                    if t % 4 == 0:
                        bp = i if t >= 8 else i - 1
                        if live(bp):
                            sums_out(bp, (t // 4 - 2) % 4)
                    if live(i):
                        exp(i, t, 0)
                        exp(i, t, 1)
                        exp(i, t, 2)
                    for name, n, b, bank in side(i, t):
                        side_step(name, n, b, bank)
                    if t == 5 and live(i - 2):
                        gate_exp(i - 2)
                    if t == 11 and live(i - 1):
                        o_hi(i - 1)

            iterations(act, one)

        @block.vector
        def _(dve):
            v = nc.vector
            k = [0]

            def step(ins):
                k[0] += 1
                ins.then_inc(s["set_dve"], 1)
                dve.wait_ge(s["set_dve"], k[0])

            dve.wait_ge(s["ld_w"], LOADS * 16)
            dve.wait_ge(s["set_act"], 1)
            step(v.tensor_scalar(c_exp, c_exp, 1.0, None, ALU.add))
            step(v.reciprocal(c_exp, c_exp))
            step(v.tensor_tensor(c_silu, c_exp, c_nat, ALU.mult))
            step(v.tensor_copy(identb[:], ident[:]))
            dve.wait_ge(s["set_pe"], 1)

            def split(hi, lo, src):
                step(v.tensor_scalar(hi, src, WS, None, ALU.mult))
                step(v.scalar_tensor_tensor(lo, src, WS, hi, ALU.mult, ALU.subtract))

            flat = ps[:].rearrange("p a b -> p (a b)")
            split(wqkv_hi[:].rearrange("p c n -> p (c n)"), wqkv_lo[:].rearrange("p c n -> p (c n)"),
                  flat[:, 0:12 * P])
            split(wo_hi[:].rearrange("p c n -> p (c n)"), wo_lo[:].rearrange("p c n -> p (c n)"),
                  flat[:, 12 * P:16 * P])
            step(v.tensor_copy(ow_t.rearrange("p c n -> p (c n)"), flat[:, 16 * P:20 * P]))
            for c in range(DC):
                split(gw_hi[:, c, :], gw_lo[:, c, :], flat[:, (20 + c) * P:(20 + c) * P + E])
                step(v.tensor_copy(c_silu_t[:, c, :], flat[:, (22 + c) * P:(22 + c) * P + NB]))
            step(v.tensor_scalar(bqk[:], b_raw, WS, None, ALU.mult))
            step(v.tensor_copy(mask_kq[:], m_nat[:, 0]))
            step(v.tensor_copy(mask_qk[:], m_nat[:, 1]))
            assert k[0] == TURNED_AT, k[0]
            dve.wait_ge(s["set_pe"], 2)
            g = ps[0:NB, 1, :]
            step(v.tensor_scalar(g_sgn, g, 0.0, 2.0, ALU.is_ge, ALU.mult))
            step(v.tensor_scalar(g_sgn, g_sgn, -1.0, None, ALU.add))
            step(v.tensor_tensor(g_abs, g, g_sgn, ALU.mult))
            step(v.tensor_scalar(g_abs, g_abs, 0.25, None, ALU.max))
            step(v.tensor_tensor(g_abs, g_abs, g_sgn, ALU.mult))
            step(v.tensor_scalar(mrow[:, 0:D], g_abs[:, 0:D], 1.0 / WS, None, ALU.mult))
            step(v.tensor_tensor(mrow[:, D:2 * D], g_abs[:, 0:D], bo_bc, ALU.mult))
            step(v.tensor_copy(mrow[:, 2 * D:3 * D], g_abs[:, D:2 * D]))
            assert k[0] == ROWS_AT, k[0]
            for n in range(4):
                src = ps[:, 0, 2 * n * NB:2 * (n + 1) * NB].rearrange("p (c b) -> p c b", c=2)
                step(v.tensor_scalar(modT[:, :, 2 * n:2 * n + 2].rearrange("p b c -> p c b"), src, 1.0 if n % 2 == 0 else 0.0, None, ALU.add))
            for c in range(DC):
                split(moe_hi[:, c, :], moe_lo[:, c, :], ps[:, 6 + c, :])
            assert k[0] == SET_DVE, k[0]
            dve.wait_ge(s["set_ready"], 3)
            dve.wait_ge(s["rows_stored"], 16)

            def stats(b, xt, st, mv, ve, nm, loaded, names, norm, rs):
                wait(dve, *loaded)
                wait(dve, norm, b * QT)
                s_st, s_ag, s_rdy = names
                for t in range(QT):
                    v.bn_stats(st[:, t, :], xt[:, t, :]).then_inc(s[s_st], 1)
                wait(dve, s_st, (b + 1) * QT, "passed_dve")
                for t in range(QT):
                    v.bn_aggr(mv[:, t, :], st[:, t, :]).then_inc(s[s_ag], 1)
                wait(dve, s_ag, (b + 1) * QT)
                wait(dve, rs, b)
                v.tensor_scalar(ve[:], mv[:, :, 1], EPS, None, ALU.add).then_inc(s[s_rdy], 1)
                v.tensor_scalar(nm[:], mv[:, :, 0], -1.0, None, ALU.mult).then_inc(s[s_rdy], 1)

            def lo_part(b, n, hf_sem, hh_sem, hl_sem, hf, hh, hl, users):
                wait(dve, hh_sem, b * 2 + n + 1)
                for name, per in users:
                    wait(dve, name, b * per)
                v.tensor_tensor(hl[:, n, :], hf[:, n, :], hh[:, n, :], ALU.subtract).then_inc(s[hl_sem], 1)

            def side_step(name, n, b, bank):
                src = ps[:, MISC + bank, :]
                if name == "ta":
                    lo_part(b, n, "hfa_ready", "hha_ready", "hla_ready", hf_a, hh_a, hl_a,
                            [("v_ready", 2), ("qk_ready", 4)])
                elif name == "t2":
                    lo_part(b, n, "hfc_ready", "hhc_ready", "hlc_ready", hf_c, hh_c, hl_c, [("moe_ready", 4)])
                elif name == "qk":
                    wait(dve, "qk_hi", b * 4 + n + 1)
                    kk = n % 2
                    v.scalar_tensor_tensor(qk_st[:, kk, 1, :], src, bqk[:, 2 * kk + n // 2:2 * kk + n // 2 + 1],
                                           qk_st[:, kk, 0, :], ALU.add, ALU.subtract).then_inc(s["qk_lo"], 1)
                elif name == "out":
                    wait(dve, "out_ready", b * 2 + n + 1)
                    wait(dve, "ga_loaded", (b + 1) * 16)
                    wait(dve, "x1_ready", b * 2)
                    v.tensor_tensor(ot[:, 2 * n:2 * n + 2, :], src.rearrange("p (u d) -> p u d", u=2),
                                    ga_bc[:, 0:1, :].broadcast_to([P, 2, D]), ALU.mult).then_inc(s["ot_ready"], 1)
                elif name == "gate":
                    gates(b, src)
                elif name == "moe":
                    wait(dve, "z0_ready", b * 4 + n + 1)
                    wait(dve, "zg_ready", b * 2)
                    v.scalar_tensor_tensor(zs[:, n, :], ps[:, MISC + bank, D:2 * D], scl[:, 1, n:n + 1], z0[:, n, :],
                                           ALU.mult, ALU.add).then_inc(s["zs_ready"], 1)

            def gates(b, src):
                N = 8

                def did(m):
                    wait(dve, "gate_step", b * N + m)
                lg = src[:, 0:QT * E].rearrange("p (t e) -> p t e", t=QT)

                def bc(a):
                    return a[:].rearrange("p (t o) -> p t o", o=1).broadcast_to([P, QT, E])
                wait(dve, "gate_ready", b + 1)
                wait(dve, "zs_ready", b * 4)
                st = s["gate_step"]
                v.tensor_reduce(gmax[:], lg, AX.X, ALU.max).then_inc(st, 1)
                did(1)
                v.tensor_tensor(gsub[:], lg, bc(gmax), ALU.subtract).then_inc(st, 1)
                wait(dve, "gate_exp", b + 1)
                v.tensor_reduce(gsum[:], gexp[:], AX.X, ALU.add).then_inc(st, 1)
                did(3)
                v.reciprocal(grec[:], gsum[:]).then_inc(st, 1)
                did(4)
                v.tensor_tensor(gp[:], gexp[:], bc(grec), ALU.mult).then_inc(st, 1)
                did(5)
                v.tensor_scalar(gtop[:], gp[:], TOP_P, None, ALU.is_gt).then_inc(st, 1)
                did(6)
                v.tensor_reduce(gcnt[:], gtop[:], AX.X, ALU.add).then_inc(st, 1)
                did(7)
                v.tensor_scalar(gcnt0[:], gcnt[:], -1.0 / WS, float(E) / WS, ALU.mult, ALU.add).then_inc(st, 1)
                did(8)
                v.tensor_tensor(scl[:, 0, :], gcnt0[:], gp[:, :, 0], ALU.mult)
                v.scalar_tensor_tensor(scl[:, 1, :], gcnt[:], 1.0 / WS, gp[:, :, 1], ALU.mult,
                                       ALU.mult).then_inc(s["scl_ready"], 1)

            def maxima(b, h, n):
                g, j = h // 4, h % 4
                if n == 0 and j == 0:
                    wait(dve, "mt_ready", b * 4 + g - 3)
                wait(dve, "mx_ready", b * 48 + 3 * h + n + 1)
                bank = MX + (3 * h + n) % 2
                col = 0
                for qt in MPART[n]:
                    w = (qt + 1) * P
                    x_ = v.tensor_reduce(mxt[:, g, 4 * j + qt:4 * j + qt + 1], ps[:, bank, col:col + w], AX.X, ALU.max)
                    col += w
                x_.then_inc(s["mx_read"], 1)

            def invert(b):
                wait(dve, "zc_loaded", (b + 1) * 16)
                wait(dve, "rz_stored", b * 16)
                v.reciprocal(zr[:], zc[:]).then_inc(s["zr_ready"], 1)

            def normalise(b):
                wait(dve, "oc_loaded", (b + 1) * 32)
                wait(dve, "rz_loaded", (b + 1) * 32)
                wait(dve, "ol_ready", b * 2)
                v.tensor_tensor(om[:], oc[:], rz[:], ALU.mult).then_inc(s["om_ready"], 1)

            def o_lo(b):
                wait(dve, "oh_ready", b * 2 + 2)
                wait(dve, "out_ready", b * 2)
                for c in range(DC):
                    v.scalar_tensor_tensor(ol[:, c, :], om[:, c, :], bv[:, c:c + 1], oh[:, c, :], ALU.add,
                                           ALU.subtract).then_inc(s["ol_ready"], 1)

            def one(i):
                for t in range(SLOTS):
                    bm, hm = max_at(i, t)
                    if live(bm):
                        maxima(bm, hm, 0)
                        maxima(bm, hm, 1)
                    for name, n, b, bank in side(i, t):
                        side_step(name, n, b, bank)
                    if t == 0 and live(i - 2):
                        stats(i - 2, x1, st_c, mv_c, ve_c, nm_c, ("x1_ready", (i - 2 + 1) * 2),
                              ("lnc_stats", "lnc_aggr", "lnc_ready"), "xnc_ready", "rsc_ready")
                    if t == 12 and live(i + 2):
                        stats(i + 2, xa, st_a, mv_a, ve_a, nm_a, ("xa_loaded", (i + 2 + 1) * 16),
                              ("lna_stats", "lna_aggr", "lna_ready"), "xna_ready", "rsa_ready")
                    if t == 7 and live(i - 1):
                        invert(i - 1)
                    if t == 11 and live(i - 1):
                        normalise(i - 1)
                        o_lo(i - 1)
                    if live(bm):
                        maxima(bm, hm, 2)

            iterations(dve, one)

        @block.gpsimd
        def _(pool):
            q = nc.gpsimd
            q.memset(kz[:], 0.0).then_inc(s["set_ready"], 1)
            q.memset(qs[:], 0.0)
            q.memset(va[:], 1.0)
            q.memset(neg_half[:], -0.5)
            q.memset(zrow[:], 0.0).then_inc(s["set_ready"], 1)
            pool.wait_ge(s["set_ready"], 2)
            q.memset(qs[0:1, :, :], QONE).then_inc(s["set_ready"], 1)
            pool.wait_ge(s["set_ready"], 3)
            pool.wait_ge(s["rows_stored"], 16)
            wait(pool, "set_dve", SET_DVE, "passed_pool")
            wait(pool, "set_pe", SET_PE, "passed_pool")

            def norm(b, xt, xn, ve, nm, rs, ready, rs_sem, xn_sem, turned_sem):
                wait(pool, ready, (b + 1) * 2, "passed_pool")
                q.tensor_tensor(rs[:], ve[:], neg_half[:], ALU.pow).then_inc(s[rs_sem], 1)
                wait(pool, rs_sem, b + 1, "passed_pool")
                wait(pool, turned_sem, b * 2, "passed_pool")
                for t in range(QT):
                    q.tensor_scalar(xn[:, t, :], xt[:, t, :], nm[:, t:t + 1], rs[:, t:t + 1], ALU.add,
                                    ALU.mult).then_inc(s[xn_sem], 1)

            def spread(b, g):
                wait(pool, "v_evicted", (b + 1) * 2, "passed_pool")
                wait(pool, "pv_done", b * 16 - 4 * (3 - g), "passed_pool")
                q.tensor_scalar(va[:, :, 4 * g:4 * g + 4, 0:HD],
                                vst[:, :, 64 * g:64 * g + 64].rearrange("p t (h d) -> p t h d", h=4),
                                1.0, 0.0, ALU.mult, ALU.add).then_inc(s["va_ready"], 1)

            def add_bias(b):
                wait(pool, "xc_loaded", (b + 1) * 16, "passed_pool")
                wait(pool, "ga_loaded", (b + 1) * 16, "passed_pool")
                wait(pool, "x1_ready", b * 2, "passed_pool")
                q.tensor_tensor(xg[:], xc[:], ga_bc[:, 1:2, :].broadcast_to([P, QT, D]), ALU.add).then_inc(s["xg_ready"], 1)

            def residual(b, n):
                wait(pool, "ot_ready", b * 2 + n + 1, "passed_pool")
                wait(pool, "xg_ready", b + 1, "passed_pool")
                wait(pool, "lnc_stats", b * QT, "passed_pool")
                wait(pool, "xnc_ready", b * QT, "passed_pool")
                wait(pool, "res_ready", b * 2, "passed_pool")
                q.tensor_tensor(x1[:, 2 * n:2 * n + 2, :], ot[:, 2 * n:2 * n + 2, :], xg[:, 2 * n:2 * n + 2, :],
                                ALU.add).then_inc(s["x1_ready"], 1)

            def finish(b, n):
                wait(pool, "zs_ready", b * 4 + 2 * n + 2, "passed_pool")
                wait(pool, "gb_loaded", (b + 1) * 16, "passed_pool")
                wait(pool, "res_ready", b * 2, "passed_pool")
                t = slice(2 * n, 2 * n + 2)
                q.tensor_tensor(zg[:, t, :], zs[:, t, :], gb_bc[:].rearrange("p (o d) -> p o d", o=1).broadcast_to([P, 2, D]),
                                ALU.mult).then_inc(s["zg_ready"], 1)
                wait(pool, "zg_ready", b * 2 + n + 1, "passed_pool")
                wait(pool, "res_stored", b * 16, "passed_pool")
                q.tensor_tensor(res[:, t, :], zg[:, t, :], x1[:, t, :], ALU.add).then_inc(s["res_ready"], 1)

            def one(i):
                if live(i - 2):
                    norm(i - 2, x1, xn_c, ve_c, nm_c, rs_c, "lnc_ready", "rsc_ready", "xnc_ready", "t2_ready")
                if live(i):
                    for g in range(3):
                        spread(i, g)
                    spread(i, 3)
                if live(i - 2):
                    finish(i - 2, 0)
                if live(i - 1):
                    add_bias(i - 1)
                if live(i - 2):
                    finish(i - 2, 1)
                if live(i + 2):
                    norm(i + 2, xa, xn_a, ve_a, nm_a, rs_a, "lna_ready", "rsa_ready", "xna_ready", "ta_ready")
                if live(i - 1):
                    residual(i - 1, 0)
                    residual(i - 1, 1)

            iterations(pool, one)


_INS = ["L0_attn_x", "L0_attn_w_qkv", "L0_attn_b_qkv", "L0_attn_w_out", "L0_attn_b_out", "L0_ffn_gate_W",
        "L0_ffn_expert_W", "L0_ffn_out_W", "L0_c", "L0_wmod"]


def constants():
    at = np.arange(P)
    later = at[:, None] > at[None, :]
    kq = np.where(later, -1e30, 0.0).astype(np.float32)
    aug = np.zeros((3, 16, 512), np.float16)
    aug[0] = np.arange(512) * (FS / QONE)
    aug[1, 0::2] = FS
    aug[2, 1::2] = FS
    return {"ident": np.eye(P, dtype=np.float32), "mask_kq": kq, "mask_qk": np.ascontiguousarray(kq.T), "kaug": aug}


def kernel(**inputs):
    import concourse.bacc as bacc
    from concourse.bass_utils import run_bass_kernel_spmd

    nc = bacc.Bacc("TRN2", target_bir_lowering=False, num_devices=1)
    arrays = {name: np.ascontiguousarray(inputs[name]) for name in _INS}
    arrays.update(constants())
    args = [nc.dram_tensor(f"in_{name}", a.shape, mybir.dt.from_np(a.dtype), kind="ExternalInput").ap()
            for name, a in arrays.items()]
    shape = arrays["L0_attn_x"].shape
    out = nc.dram_tensor("out_0", shape, F32, kind="ExternalOutput").ap()
    build(nc, *args, out)
    r = run_bass_kernel_spmd(nc, [{f"in_{name}": a for name, a in arrays.items()}], core_ids=[0])
    return r.results[0]["out_0"]
```

```python
from contextlib import ExitStack

import numpy as np

import concourse.bass as bass
from concourse import mybir

F32 = mybir.dt.float32
F16 = mybir.dt.float16
BF16 = mybir.dt.bfloat16
ALU = mybir.AluOpType
ACT = mybir.ActivationFunctionType
AX = mybir.AxisListType

P = 128
WS = 16.0
FS = 4 * WS * WS
QONE = 64.0
EPS = 1e-5
TOP_P = 0.3
SLOTS = 16
PE_ORDER = "01a2sbwc"
ACT_ORDER = "0s12"
DVE_ORDER = "Saboc"
LOADS = 13
TURNED_AT, ROWS_AT, SET_DVE = 17, 25, 33
SET_PE = 2
AUG = 18
STACK_DMAS = 10


def build(nc, x, w_qkv, b_qkv, w_out, b_out, gate_w, expert_w, out_w, cond, wmod,
          ident_d, mask_qk_d, kaug_d, qaug_d, out):
    NB, S, D = x.shape
    H, HD = 16, 16
    QT = S // P
    DC = D // P
    E = gate_w.shape[0]
    HP = H // 2
    assert (S, D, QT, DC) == (512, 256, 4, 2) and E == 8

    ctx = ExitStack()
    with ctx:
        def sb(name, shape, dt):
            return ctx.enter_context(nc.sbuf_tensor(name, shape, dt))

        def sem(name):
            return ctx.enter_context(nc.semaphore(name))

        def dram(name, shape, dt):
            return nc.dram_tensor(name, shape, dt, kind="Internal").ap()

        ps = ctx.enter_context(nc.psum_tensor("ps", [P, 8, 512], F32))
        ST, MX, PVB, MISC = 0, 3, 5, 6

        ident = sb("ident", [P, P], F32)
        identb = sb("identb", [P, P], BF16)
        mask_qk = sb("mask_qk", [P, P], BF16)
        wqkv_hi = sb("wqkv_hi", [P, DC, 3 * D], F16)
        wqkv_lo = sb("wqkv_lo", [P, DC, 3 * D], F16)
        wo_hi = sb("wo_hi", [P, DC, D], F16)
        wo_lo = sb("wo_lo", [P, DC, D], F16)
        moe_hi = sb("moe_hi", [P, DC, 2 * D], F16)
        moe_lo = sb("moe_lo", [P, DC, 2 * D], F16)
        gw_hi = sb("gw_hi", [P, DC, E], F16)
        gw_lo = sb("gw_lo", [P, DC, E], F16)
        bqk = sb("bqk", [P, 4], F32)
        bv = sb("bv", [P, DC], F32)
        modT = sb("modT", [P, NB, 8], F32)
        zrow = sb("zrow", [2, 2 * S], F16)

        qs = sb("qs", [P, HP, S], F16)
        kz = sb("kz", [P, H, S], F16)
        prob = sb("prob", [P, 8, 10 * P], F32)
        va = sb("va", [P, QT, H, 32], F32)
        vst = sb("vst", [P, QT, D], F32)
        mxt = sb("mxt", [P, 4, QT, 4], F32)
        negm = sb("negm", [4, S], F16)
        xa = sb("xa", [P, QT, D], F32)
        xn_a = sb("xn_a", [P, QT, D], F32)
        mod_a = sb("mod_a", [P, 4], F32)
        st_a = sb("st_a", [P, QT, 6], F32)
        mv_a = sb("mv_a", [P, QT, 2], F32)
        ve_a = sb("ve_a", [P, QT], F32)
        nm_a = sb("nm_a", [P, QT], F32)
        rs_a = sb("rs_a", [P, QT], F32)
        hf_a = sb("hf_a", [P, DC, S], F32)
        hh_a = sb("hh_a", [P, DC, S], F16)
        hl_a = sb("hl_a", [P, DC, S], F16)
        qk_st = sb("qk_st", [P, 2, 2, S], F16)
        ou = sb("ou", [P, 4, S], F32)
        oc = sb("oc", [P, DC, S], F32)
        zc = sb("zc", [64, P], F32)
        zr = sb("zr", [64, P], F32)
        rz = sb("rz", [P, DC, S], F32)
        om = sb("om", [P, DC, S], F32)
        oh = sb("oh", [P, DC, S], F16)
        ol = sb("ol", [P, DC, S], F16)
        xc = sb("xc", [P, QT, D], F32)
        xg = sb("xg", [P, QT, D], F32)
        ga_bc = sb("ga_bc", [P, 2, D], F32)
        gb_bc = sb("gb_bc", [P, D], F32)
        ot = sb("ot", [P, QT, D], F32)
        x1 = sb("x1", [P, QT, D], F32)
        xn_c = sb("xn_c", [P, QT, D], F32)
        mod_c = sb("mod_c", [P, 4], F32)
        st_c = sb("st_c", [P, QT, 6], F32)
        mv_c = sb("mv_c", [P, QT, 2], F32)
        ve_c = sb("ve_c", [P, QT], F32)
        nm_c = sb("nm_c", [P, QT], F32)
        rs_c = sb("rs_c", [P, QT], F32)
        hf_c = sb("hf_c", [P, DC, S], F32)
        hh_c = sb("hh_c", [P, DC, S], F16)
        hl_c = sb("hl_c", [P, DC, S], F16)
        gmax = sb("gmax", [P, QT], F32)
        gsub = sb("gsub", [P, QT, E], F32)
        gexp = sb("gexp", [P, QT, E], F32)
        gsum = sb("gsum", [P, QT], F32)
        grec = sb("grec", [P, QT], F32)
        gp = sb("gp", [P, QT, E], F32)
        gtop = sb("gtop", [P, QT, E], F32)
        gcnt = sb("gcnt", [P, QT], F32)
        gcnt0 = sb("gcnt0", [P, QT], F32)
        scl = sb("scl", [P, 2, QT], F32)
        z0 = sb("z0", [P, QT, D], F32)
        zs = sb("zs", [P, QT, D], F32)
        zg = sb("zg", [P, QT, D], F32)
        res = sb("res", [P, QT, D], F32)
        neg_half = sb("neg_half", [P, QT], F32)

        spare = prob[:].rearrange("p a b -> p (a b)")
        taken = [0]

        def lend(rows, *dims):
            size = int(np.prod(dims))
            got = spare[0:rows, taken[0]:taken[0] + size]
            taken[0] += size
            if len(dims) == 2:
                got = got.rearrange("p (a b) -> p a b", a=dims[0])
            if len(dims) == 3:
                got = got.rearrange("p (a b c) -> p a b c", a=dims[0], b=dims[1])
            return got

        wq_nat, wo_nat, ow_nat = lend(P, 6, D), lend(P, DC, D), lend(P, DC, D)
        ex_nat, g_nat, c_nat = lend(P, 2, DC, D), lend(E, D), lend(NB, D)
        wm_nat, b_raw, bo_bc = lend(P, DC, 6 * D), lend(P, 4), lend(NB, D)
        c_exp, c_silu, c_silu_t = lend(NB, D), lend(NB, D), lend(P, DC, NB)
        g_sgn, g_abs, mrow = lend(NB, 2 * D), lend(NB, 2 * D), lend(NB, 3 * D)
        m_nat = lend(P, P)
        ow_t = vst[:, 0:2, :]

        qk_d = dram("qk_d", [2, 2, 2, P, S], F16)
        ou_d = dram("ou_d", [4 * P, S], F32)
        rz_d = dram("rz_d", [H, S], F32)
        rows_d = dram("rows_d", [NB, 3 * D], F32)

        block = ctx.enter_context(nc.Block())
        s = {}

        def sm(name):
            if name not in s:
                s[name] = sem(name)
            return s[name]

        for name in ("ld_w", "set_dve", "set_pe", "set_act", "set_ready", "rows_stored", "kaug_loaded",
                     "xa_loaded", "moda_loaded", "lna_stats", "lna_aggr", "lna_ready", "rsa_ready", "xna_ready",
                     "ta_ready", "hfa_ready", "hha_ready", "hla_ready", "qk_ready", "qk_hi", "qk_lo",
                     "qk_stored0", "qk_stored1", "qk_stored2", "qk_stored3", "stack_loaded0", "stack_loaded1",
                     "stack_loaded2", "stack_loaded3", "masked",
                     "v_ready", "v_evicted", "va_ready", "mx_ready", "mx_read", "mt_ready", "nm_ready",
                     "aug_loaded", "st_ready", "exp_done", "pv_done", "ou_ready", "ou_stored",
                     "zc_loaded", "oc_loaded", "zr_ready", "rz_stored", "rz_loaded", "om_ready", "oh_ready",
                     "ol_ready", "out_ready", "ot_ready", "x1_ready", "xc_loaded", "ga_loaded", "xg_ready",
                     "lnc_stats", "lnc_aggr", "lnc_ready", "rsc_ready", "xnc_ready", "modc_loaded", "gb_loaded",
                     "t2_ready", "hfc_ready", "hhc_ready", "hlc_ready", "gate_ready", "gate_step", "gate_exp",
                     "scl_ready", "moe_ready", "z0_ready", "zs_ready", "zg_ready", "res_ready", "res_stored",
                     "passed_sp", "passed_dve", "passed_pool"):
            sm(name)

        def wait(eng, name, value, passed=None):
            if isinstance(value, int) and value <= 0:
                return
            eng.wait_ge(s[name], value)
            if passed and not isinstance(value, int):
                eng.sem_inc(s[passed], 1)

        SIDE = {
            0: [("ta", 0, 1, 1), ("ta", 1, 1, 0)],
            1: [("mt", 1, 0, 1)],
            2: [("qk", 0, 1, 1)],
            3: [("qk", 1, 1, 0)],
            4: [("t2", 0, -2, 1), ("t2", 1, -2, 0)],
            5: [("mt", 2, 0, 1), ("v", 0, 1, 0)],
            6: [("gate", 0, -2, 1)],
            7: [("moe", 0, -2, 0)],
            8: [("qk", 2, 1, 1)],
            9: [("qk", 3, 1, 0), ("mt", 3, 0, 1)],
            10: [("moe", 1, -2, 1)],
            11: [("moe", 2, -2, 0)],
            12: [("moe", 3, -2, 1)],
            13: [("mt", 0, 1, 0), ("v", 1, 1, 0)],
            14: [("out", 0, -1, 1)],
            15: [("out", 1, -1, 0)],
        }
        READ = {"ta": ("hha_ready", 2), "qk": ("qk_lo", 4), "mt": ("nm_ready", 4), "t2": ("hhc_ready", 2),
                "gate": ("gate_step", 8), "moe": ("zs_ready", 4), "v": ("v_evicted", 2), "out": ("ot_ready", 2)}

        def live(b):
            return not isinstance(b, int) or 0 <= b < NB

        def iterations(eng, one, first=-2):
            for i in range(first, 2):
                one(i)
            with eng.Fori(2, NB - 2) as i:
                one(i)
            for i in range(NB - 2, NB + 2):
                one(i)

        def side(i, t):
            for name, n, off, bank in SIDE.get(t, []):
                if live(i + off):
                    yield name, n, i + off, bank

        def before(i, t, pos, bank):
            order = [(u, q, st) for u in sorted(SIDE) for q, st in enumerate(SIDE[u])]
            at = [n for n, (u, q, _) in enumerate(order) if (u, q) == (t, pos)][0]
            for back in range(1, 3 * len(order)):
                laps, n = divmod(at - back, len(order))
                name, idx, off, bk = order[n][2]
                if bk == bank and live(i + off + laps):
                    return name, idx, i + off + laps
                if bk == bank and isinstance(i, int) and i + off + laps < 0 and laps < -1:
                    return None
            return None

        def max_at(i, t):
            return (i + 1, t - 8) if t >= 8 else (i, t + 8)

        CHUNK = [[(0, 0, 1), (1, 1, 1), (2, 2, 1), (3, 3, 1)], [(0, 1, 3), (2, 3, 1)], [(1, 2, 2)]]
        PCOL = {0: 4 * P, 1: 8 * P, 2: 7 * P}
        MPART = [[3], [2, 0], [1]]

        @block.sync
        def _(sp):
            n = [0]

            def ld(dst, src, **kw):
                sp.dma_start(dst, src, **kw).then_inc(s["ld_w"], 16)
                n[0] += 1
            ld(ident[:], ident_d)
            ld(wq_nat, w_qkv.rearrange("(k p) d -> p k d", p=P))
            ld(wo_nat, w_out.rearrange("(k p) d -> p k d", p=P))
            ld(ow_nat, out_w.rearrange("(k p) d -> p k d", p=P))
            for e in range(2):
                ld(ex_nat[:, e], expert_w[e].rearrange("(k p) d -> p k d", p=P))
            ld(g_nat, gate_w)
            ld(c_nat, cond)
            ld(wm_nat, wmod.rearrange("(k p) n -> p k n", p=P))
            ld(m_nat, mask_qk_d)
            ld(b_raw, b_qkv[0:2 * D].rearrange("(c p) -> p c", p=P), allow_slow_non_contiguous=True)
            ld(bv[:], b_qkv[2 * D:3 * D].rearrange("(c p) -> p c", p=P), allow_slow_non_contiguous=True)
            ld(bo_bc, b_out.rearrange("(o d) -> o d", o=1).broadcast_to([NB, D]))
            assert n[0] == LOADS, n[0]
            sp.wait_ge(s["set_ready"], 2)
            sp.dma_start(kz[0:AUG, :, :], kaug_d).then_inc(s["kaug_loaded"], 16)
            sp.dma_start(qs[0:AUG, :, :], qaug_d).then_inc(s["kaug_loaded"], 16)
            wait(sp, "set_dve", ROWS_AT, "passed_sp")
            sp.dma_start(rows_d, mrow).then_inc(s["rows_stored"], 16)
            sp.wait_ge(s["rows_stored"], 16)
            sp.wait_ge(s["kaug_loaded"], 32)
            wait(sp, "set_dve", SET_DVE, "passed_sp")
            wait(sp, "set_pe", SET_PE, "passed_sp")
            wait(sp, "set_ready", 2, "passed_sp")

            def load_a(b):
                wait(sp, "xna_ready", b * QT, "passed_sp")
                sp.dma_start(xa[:], x[b].rearrange("(t p) d -> p t d", p=P)).then_inc(s["xa_loaded"], 16)
                wait(sp, "hha_ready", b * 2, "passed_sp")
                sp.dma_start(mod_a[:], modT[:, b, 0:4]).then_inc(s["moda_loaded"], 16)

            def store_qk(b, n):
                wait(sp, "qk_lo", b * 4 + n + 1, "passed_sp")
                for g in (n // 2 * 2, n // 2 * 2 + 1):
                    wait(sp, f"stack_loaded{g}", b * STACK_DMAS * 16, "passed_sp")
                sp.dma_start(qk_d[n % 2, n // 2].rearrange("l p t -> p l t"), qk_st[:, n % 2]).then_inc(
                    s[f"qk_stored{n}"], 16)

            def load_stack(b, g):
                c, at = g // 2, 64 * (g % 2)
                wait(sp, f"qk_stored{2 * c}", (b + 1) * 16, "passed_sp")
                wait(sp, f"qk_stored{2 * c + 1}", (b + 1) * 16, "passed_sp")
                wait(sp, "st_ready", b * 48 - 48 + 12 * (g + 1), "passed_sp")
                done = s[f"stack_loaded{g}"]
                pr = slice(2 * g, 2 * g + 2)
                sp.dma_start(qs[1:3, pr, :], zrow[:].rearrange("p (a t) -> p a t", a=2)).then_inc(done, 16)
                for r, part in enumerate((0, 0, 1)):
                    sp.dma_start(qs[32 * (r + 1):32 * (r + 2), pr, :],
                                 qk_d[0, c, part, at:at + 64, :].rearrange("(a r) t -> r a t", a=2)).then_inc(done, 16)
                for r, part in enumerate((0, 1, 0)):
                    for j in range(2):
                        lo = 32 * (r + 1) + 16 * j
                        sp.dma_start(kz[lo:lo + 16, 4 * g + j:4 * g + 4:2, :],
                                     qk_d[1, c, part, at:at + 64, :].rearrange("(a j r) t -> j r a t", a=2, j=2)[j]
                                     ).then_inc(done, 16)

            def load_aug(b, g):
                wait(sp, "nm_ready", b * 4 + g + 1, "passed_sp")
                for a in range(2):
                    sp.dma_start(qs[1:3, 2 * g + a, :], negm[2 * a:2 * a + 2, :]).then_inc(s["aug_loaded"], 16)

            def store_ou(b, g):
                wait(sp, "ou_ready", b * 4 + g + 1, "passed_sp")
                wait(sp, "oc_loaded", b * 32, "passed_sp")
                wait(sp, "zc_loaded", b * 16, "passed_sp")
                sp.dma_start(ou_d[P * g:P * (g + 1), :], ou[:, g, :]).then_inc(s["ou_stored"], 16)

            def load_o(b):
                wait(sp, "ou_stored", (b + 1) * 64, "passed_sp")
                wait(sp, "zr_ready", b, "passed_sp")
                sp.dma_start(zc[:], ou_d.rearrange("(h r) (u t) -> h r u t", r=32, u=4)[:, 16]).then_inc(
                    s["zc_loaded"], 16)
                wait(sp, "om_ready", b, "passed_sp")
                for c in range(DC):
                    src = ou_d.rearrange("(c h r) t -> c h r t", c=DC, r=32)[c, :, 0:HD, :]
                    sp.dma_start(oc[:, c, :], src).then_inc(s["oc_loaded"], 16)

            def store_rz(b):
                wait(sp, "zr_ready", b + 1, "passed_sp")
                wait(sp, "rz_loaded", b * 32, "passed_sp")
                sp.dma_start(rz_d.rearrange("h (u t) -> (h u) t", u=4), zr[:]).then_inc(s["rz_stored"], 16)

            def load_rz(b):
                wait(sp, "rz_stored", (b + 1) * 16, "passed_sp")
                for c in range(DC):
                    src = rz_d[8 * c:8 * c + 8, :].rearrange("h (o t) -> h o t", o=1).broadcast_to([8, HD, S])
                    sp.dma_start(rz[:, c, :], src).then_inc(s["rz_loaded"], 16)

            def load_c(b):
                wait(sp, "xg_ready", b, "passed_sp")
                sp.dma_start(xc[:], x[b].rearrange("(t p) d -> p t d", p=P)).then_inc(s["xc_loaded"], 16)

            def load_ga(b):
                wait(sp, "ot_ready", b * 2, "passed_sp")
                src = rows_d[bass.ds(b, 1), 0:2 * D].rearrange("o (k d) -> o k d", k=2).broadcast_to([P, 2, D])
                sp.dma_start(ga_bc[:], src).then_inc(s["ga_loaded"], 16)

            def load_gb(b):
                wait(sp, "zg_ready", b * 2, "passed_sp")
                sp.dma_start(gb_bc[:], rows_d[bass.ds(b, 1), 2 * D:3 * D].broadcast_to([P, D])).then_inc(
                    s["gb_loaded"], 16)

            def load_modc(b):
                wait(sp, "hhc_ready", b * 2, "passed_sp")
                sp.dma_start(mod_c[:], modT[:, b, 4:8]).then_inc(s["modc_loaded"], 16)

            def store_res(b):
                wait(sp, "res_ready", (b + 1) * 2, "passed_sp")
                sp.dma_start(out[b].rearrange("(t p) d -> p t d", p=P), res[:]).then_inc(s["res_stored"], 16)

            SP = {
                0: [(load_stack, 3, 0), (store_ou, 2, -1)],
                1: [(load_gb, None, -2)],
                2: [(load_aug, 1, 0), (load_c, None, -1)],
                3: [(store_qk, 0, 1), (load_a, None, 2)],
                4: [(store_qk, 1, 1), (store_ou, 3, -1)],
                5: [(load_stack, 0, 1), (load_o, None, -1)],
                6: [(load_aug, 2, 0), (load_ga, None, -1)],
                7: [(store_rz, None, -1)],
                8: [(load_stack, 1, 1), (load_rz, None, -1), (store_ou, 0, 0)],
                9: [(store_qk, 2, 1)],
                10: [(load_aug, 3, 0), (store_qk, 3, 1)],
                12: [(load_stack, 2, 1), (store_ou, 1, 0), (load_modc, None, -1)],
                14: [(load_aug, 0, 1), (store_res, None, -2)],
            }

            def one(i):
                for t in range(SLOTS):
                    for f, n, off in SP.get(t, []):
                        if live(i + off):
                            f(*([i + off] if n is None else [i + off, n]))

            iterations(sp, one)
            wait(sp, "res_stored", NB * 16, "passed_sp")

        @block.tensor
        def _(pe):
            mm = nc.tensor.matmul

            pe.wait_ge(s["ld_w"], LOADS * 16)

            def turn(n, src, rows=P):
                return nc.tensor.transpose(ps[:, n // 4, (n % 4) * P:(n % 4) * P + rows], src, ident[0:rows, 0:rows])

            for c in range(DC):
                for k in range(6):
                    turn(c * 6 + k, wq_nat[:, k, c * P:(c + 1) * P])
                for k in range(DC):
                    turn(12 + c * 2 + k, wo_nat[:, k, c * P:(c + 1) * P])
                    turn(16 + c * 2 + k, ow_nat[:, k, c * P:(c + 1) * P])
            pe.wait_ge(s["set_act"], 1)
            pe.wait_ge(s["set_dve"], 4)
            for c in range(DC):
                turn(20 + c, g_nat[:, c * P:(c + 1) * P], E)
                x_ = turn(22 + c, c_silu[:, c * P:(c + 1) * P], NB)
            x_.then_inc(s["set_pe"], 1)
            pe.wait_ge(s["set_dve"], TURNED_AT)
            for c in range(DC):
                for e in range(2):
                    for k in range(DC):
                        mm(ps[:, 6 + c, e * D:(e + 1) * D], ex_nat[:, e, k, c * P:(c + 1) * P],
                           ow_t[:, k, :], start=(k == 0), stop=(k == DC - 1))
            for n, part in enumerate((1, 0, 4, 3)):
                for c in range(DC):
                    for k in range(DC):
                        col = part * D + c * P
                        mm(ps[:, 0, (2 * n + c) * NB:(2 * n + c + 1) * NB], wm_nat[:, k, col:col + P],
                           c_silu_t[:, k, :], start=(k == 0), stop=(k == DC - 1))
            for n, part in enumerate((2, 5)):
                for k in range(DC):
                    x_ = mm(ps[0:NB, 1, n * D:(n + 1) * D], c_silu_t[:, k, :],
                            wm_nat[:, k, part * D:(part + 1) * D], start=(k == 0), stop=(k == DC - 1))
            x_.then_inc(s["set_pe"], 1)
            pe.wait_ge(s["set_dve"], SET_DVE)
            pe.wait_ge(s["set_ready"], 2)
            pe.wait_ge(s["kaug_loaded"], 32)

            def products(dst, pairs, last_sem=None):
                for n, (a, b) in enumerate(pairs):
                    x_ = mm(dst, a, b, start=(n == 0), stop=(n == len(pairs) - 1))
                return x_

            def side_step(name, n, b, bank, prev):
                if prev is not None:
                    pname, pn, pb = prev
                    rd, per = READ[pname]
                    wait(pe, rd, pb * per + (2 if pname == "gate" else pn + 1))
                dst = ps[:, MISC + bank, :]
                if name == "ta":
                    wait(pe, "xna_ready", (b + 1) * QT)
                    for t in range(QT):
                        x_ = nc.tensor.transpose(dst[:, t * P:(t + 1) * P], xn_a[:, t, n * P:(n + 1) * P], ident[:])
                    x_.then_inc(s["ta_ready"], 1)
                elif name == "t2":
                    wait(pe, "xnc_ready", (b + 1) * QT)
                    for t in range(QT):
                        x_ = nc.tensor.transpose(dst[:, t * P:(t + 1) * P], xn_c[:, t, n * P:(n + 1) * P], ident[:])
                    x_.then_inc(s["t2_ready"], 1)
                elif name == "qk":
                    wait(pe, "hla_ready", (b + 1) * 2)
                    col = (n % 2) * D + (n // 2) * P
                    w = slice(col, col + P)
                    pairs = []
                    for c in range(DC):
                        pairs += [(wqkv_hi[:, c, w], hh_a[:, c, :]), (wqkv_hi[:, c, w], hl_a[:, c, :]),
                                  (wqkv_lo[:, c, w], hh_a[:, c, :])]
                    products(dst, pairs).then_inc(s["qk_ready"], 1)
                elif name == "v":
                    for u in range(2):
                        t = slice((2 * n + u) * P, (2 * n + u + 1) * P)
                        pairs = []
                        for c in range(DC):
                            pairs += [(hh_a[:, c, t], wqkv_hi[:, c, 2 * D:]), (hh_a[:, c, t], wqkv_lo[:, c, 2 * D:]),
                                      (hl_a[:, c, t], wqkv_hi[:, c, 2 * D:])]
                        x_ = products(dst[:, u * D:(u + 1) * D], pairs)
                    x_.then_inc(s["v_ready"], 1)
                elif name == "mt":
                    wait(pe, "mx_read", b * 48 + 12 * (n + 1))
                    for t in range(QT):
                        x_ = nc.tensor.transpose(dst[0:4, t * P:(t + 1) * P], mxt[:, n, t, :], ident[:])
                    x_.then_inc(s["mt_ready"], 1)
                elif name == "out":
                    wait(pe, "ol_ready", (b + 1) * 2)
                    for u in range(2):
                        t = slice((2 * n + u) * P, (2 * n + u + 1) * P)
                        pairs = []
                        for c in range(DC):
                            pairs += [(oh[:, c, t], wo_hi[:, c, :]), (oh[:, c, t], wo_lo[:, c, :]),
                                      (ol[:, c, t], wo_hi[:, c, :])]
                        x_ = products(dst[:, u * D:(u + 1) * D], pairs)
                    x_.then_inc(s["out_ready"], 1)
                elif name == "gate":
                    wait(pe, "hlc_ready", (b + 1) * 2)
                    for u in range(QT):
                        t = slice(u * P, (u + 1) * P)
                        pairs = []
                        for c in range(DC):
                            pairs += [(hh_c[:, c, t], gw_hi[:, c, :]), (hh_c[:, c, t], gw_lo[:, c, :]),
                                      (hl_c[:, c, t], gw_hi[:, c, :])]
                        x_ = products(dst[:, u * E:(u + 1) * E], pairs)
                    x_.then_inc(s["gate_ready"], 1)
                elif name == "moe":
                    t = slice(n * P, (n + 1) * P)
                    pairs = []
                    for c in range(DC):
                        pairs += [(hh_c[:, c, t], moe_hi[:, c, :]), (hh_c[:, c, t], moe_lo[:, c, :]),
                                  (hl_c[:, c, t], moe_hi[:, c, :])]
                    products(dst, pairs).then_inc(s["moe_ready"], 1)

            def scores(b, h, n):
                if h % 4 == 0 and n == 0:
                    wait(pe, "aug_loaded", (b * 4 + h // 4 + 1) * 32)
                wait(pe, "exp_done", b * 48 + 3 * h + n - 2)
                col = 0
                for kt, qt, w in CHUNK[n]:
                    x_ = mm(ps[:, ST + n, col:col + w * P], kz[:, h, kt * P:(kt + 1) * P],
                            qs[:, h // 2, qt * P:(qt + w) * P], start=True, stop=True)
                    col += w * P
                x_.then_inc(s["st_ready"], 1)

            def row_scores(b, h, n):
                if h % 4 == 0 and n == 0:
                    wait(pe, f"stack_loaded{h // 4}", (b + 1) * STACK_DMAS * 16)
                wait(pe, "mx_read", b * 48 + 3 * h + n - 1)
                bank = MX + (3 * h + n) % 2
                col = 0
                for qt in MPART[n]:
                    w = (qt + 1) * P
                    mm(ps[:, bank, col:col + w], qs[:, h // 2, qt * P:(qt + 1) * P], kz[:, h, 0:w],
                       start=True, stop=False)
                    x_ = mm(ps[:, bank, col + w - P:col + w], identb[:], mask_qk[:], start=False, stop=True)
                    col += w
                x_.then_inc(s["mx_ready"], 1)

            def weigh(b, g, kt):
                if kt == 0:
                    wait(pe, "exp_done", b * 48 + 12 * (g + 1))
                    wait(pe, "masked", b * 16 + 4 * (g + 1))
                    wait(pe, "va_ready", b * 4 + g + 1)
                    wait(pe, "ou_ready", b * 4 + g)
                for j in range(4):
                    h = 4 * g + j
                    x_ = mm(ps[32 * j:32 * j + 32, PVB, kt * P:(kt + 1) * P], va[:, kt, h, :],
                            prob[:, h % 8, kt * P:(kt + 1) * P], start=(kt == 0), stop=(kt == QT - 1))
                if kt < QT - 1:
                    for j in range(4):
                        h = 4 * g + j
                        w = (QT - 1 - kt) * P
                        x_ = mm(ps[32 * j:32 * j + 32, PVB, (kt + 1) * P:S], va[:, kt, h, :],
                                prob[:, h % 8, PCOL[kt]:PCOL[kt] + w], start=False, stop=False)
                x_.then_inc(s["pv_done"], 1)

            def one(i):
                for t in range(SLOTS):
                    bm, hm = max_at(i, t)
                    bp = i if t >= 4 else i - 1
                    for what in PE_ORDER:
                        if what in "012" and live(i):
                            scores(i, t, int(what))
                        if what in "abc" and live(bm):
                            row_scores(bm, hm, "abc".index(what))
                        if what == "s":
                            for pos, (name, n, off, bank) in enumerate(SIDE.get(t, [])):
                                if live(i + off):
                                    side_step(name, n, i + off, bank, before(i, t, pos, bank))
                        if what == "w" and live(bp):
                            weigh(bp, (t // 4 - 1) % 4, t % 4)

            iterations(pe, one)

        @block.scalar
        def _(act):
            act.wait_ge(s["ld_w"], LOADS * 16)
            nc.scalar.activation(c_exp, c_nat, ACT.Exp, scale=-1.0).then_inc(s["set_act"], 1)
            wait(act, "set_dve", SET_DVE)
            wait(act, "set_ready", 2)
            wait(act, "rows_stored", 16)

            def exp(b, h, n):
                if n == 0 and h % 4 == 0:
                    wait(act, "pv_done", b * 16 + h - 4)
                wait(act, "st_ready", b * 48 + 3 * h + n + 1)
                at, w = [(0, 512), (512, 512), (1024, 256)][n]
                nc.scalar.activation(prob[:, h % 8, at:at + w], ps[:, ST + n, 0:w], ACT.Exp,
                                     scale=1.0 / FS).then_inc(s["exp_done"], 1)

            def turned(b, n, bank, ready, mod, loaded, hf, hh, hf_sem, hh_sem, hl_sem, users):
                wait(act, ready, b * 2 + n + 1)
                wait(act, loaded, (b + 1) * 16)
                wait(act, hl_sem, b * 2)
                for name, per in users:
                    wait(act, name, b * per)
                src = ps[:, MISC + bank, :]
                nc.scalar.activation(hf[:, n, :], src, ACT.Identity, bias=mod[:, 2 + n:3 + n],
                                     scale=mod[:, n:n + 1]).then_inc(s[hf_sem], 1)
                nc.scalar.activation(hh[:, n, :], src, ACT.Identity, bias=mod[:, 2 + n:3 + n],
                                     scale=mod[:, n:n + 1]).then_inc(s[hh_sem], 1)

            def side_step(name, n, b, bank):
                src = ps[:, MISC + bank, :]
                if name == "ta":
                    turned(b, n, bank, "ta_ready", mod_a, "moda_loaded", hf_a, hh_a, "hfa_ready", "hha_ready",
                           "hla_ready", [("v_ready", 2), ("qk_ready", 4)])
                elif name == "t2":
                    turned(b, n, bank, "t2_ready", mod_c, "modc_loaded", hf_c, hh_c, "hfc_ready", "hhc_ready",
                           "hlc_ready", [("moe_ready", 4)])
                elif name == "qk":
                    wait(act, "qk_ready", b * 4 + n + 1)
                    k = n % 2
                    if n >= 2:
                        wait(act, f"qk_stored{n - 2}", (b + 1) * 16)
                    else:
                        wait(act, f"qk_stored{n + 2}", b * 16)
                    nc.scalar.activation(qk_st[:, k, 0, :], src, ACT.Identity,
                                         bias=bqk[:, 2 * k + n // 2:2 * k + n // 2 + 1]).then_inc(s["qk_hi"], 1)
                elif name == "v":
                    wait(act, "v_ready", b * 2 + n + 1)
                    wait(act, "va_ready", b * 4)
                    nc.scalar.activation(vst[:, 2 * n:2 * n + 2, :], src.rearrange("p (u d) -> p u d", u=2),
                                         ACT.Copy, scale=1.0 / WS).then_inc(s["v_evicted"], 1)
                elif name == "mt":
                    wait(act, "mt_ready", b * 4 + n + 1)
                    wait(act, "aug_loaded", (b * 4 + n) * 32)
                    nc.scalar.activation(negm[:], ps[0:4, MISC + bank, :], ACT.Copy,
                                         scale=-1.0 / FS).then_inc(s["nm_ready"], 1)
                elif name == "moe":
                    wait(act, "moe_ready", b * 4 + n + 1)
                    wait(act, "scl_ready", b + 1)
                    wait(act, "zs_ready", b * 4)
                    nc.scalar.activation(z0[:, n, :], ps[:, MISC + bank, 0:D], ACT.Copy,
                                         scale=scl[:, 0, n:n + 1]).then_inc(s["z0_ready"], 1)

            def sums_out(b, g):
                wait(act, "pv_done", b * 16 + 4 * g + 4)
                if g == 0:
                    wait(act, "ou_stored", b * 64)
                nc.scalar.activation(ou[:, g, :], ps[:, PVB, :], ACT.Copy).then_inc(s["ou_ready"], 1)

            def gate_exp(b):
                wait(act, "gate_step", b * 8 + 2)
                wait(act, "gate_step", b * 8)
                nc.scalar.activation(gexp[:], gsub[:], ACT.Exp, scale=1.0 / WS).then_inc(s["gate_exp"], 1)

            def o_hi(b):
                wait(act, "om_ready", b + 1)
                wait(act, "out_ready", b * 2)
                wait(act, "ol_ready", b * 2)
                for c in range(DC):
                    nc.scalar.activation(oh[:, c, :], om[:, c, :], ACT.Identity,
                                         bias=bv[:, c:c + 1]).then_inc(s["oh_ready"], 1)

            def one(i):
                for t in range(SLOTS):
                    if t % 4 == 0:
                        bp = i if t >= 8 else i - 1
                        if live(bp):
                            sums_out(bp, (t // 4 - 2) % 4)
                    for what in ACT_ORDER:
                        if what in "012" and live(i):
                            exp(i, t, int(what))
                        if what == "s":
                            for name, n, b, bank in side(i, t):
                                side_step(name, n, b, bank)
                        if what == "S":
                            for name, n, b, bank in side(*((i, t - 1) if t else (i - 1, SLOTS - 1))):
                                side_step(name, n, b, bank)
                    if t == 6 and live(i - 2):
                        gate_exp(i - 2)
                    if t == 10 and live(i - 1):
                        o_hi(i - 1)

            iterations(act, one)

        @block.vector
        def _(dve):
            v = nc.vector
            k = [0]

            def step(ins):
                k[0] += 1
                ins.then_inc(s["set_dve"], 1)
                dve.wait_ge(s["set_dve"], k[0])

            dve.wait_ge(s["ld_w"], LOADS * 16)
            dve.wait_ge(s["set_act"], 1)
            step(v.tensor_scalar(c_exp, c_exp, 1.0, None, ALU.add))
            step(v.reciprocal(c_exp, c_exp))
            step(v.tensor_tensor(c_silu, c_exp, c_nat, ALU.mult))
            step(v.tensor_copy(identb[:], ident[:]))
            dve.wait_ge(s["set_pe"], 1)

            def split(hi, lo, src):
                step(v.tensor_scalar(hi, src, WS, None, ALU.mult))
                step(v.scalar_tensor_tensor(lo, src, WS, hi, ALU.mult, ALU.subtract))

            flat = ps[:].rearrange("p a b -> p (a b)")
            split(wqkv_hi[:].rearrange("p c n -> p (c n)"), wqkv_lo[:].rearrange("p c n -> p (c n)"),
                  flat[:, 0:12 * P])
            split(wo_hi[:].rearrange("p c n -> p (c n)"), wo_lo[:].rearrange("p c n -> p (c n)"),
                  flat[:, 12 * P:16 * P])
            step(v.tensor_copy(ow_t.rearrange("p c n -> p (c n)"), flat[:, 16 * P:20 * P]))
            for c in range(DC):
                split(gw_hi[:, c, :], gw_lo[:, c, :], flat[:, (20 + c) * P:(20 + c) * P + E])
                step(v.tensor_copy(c_silu_t[:, c, :], flat[:, (22 + c) * P:(22 + c) * P + NB]))
            step(v.tensor_scalar(bqk[:], b_raw, WS, None, ALU.mult))
            step(v.tensor_copy(mask_qk[:], m_nat))
            assert k[0] == TURNED_AT, k[0]
            dve.wait_ge(s["set_pe"], 2)
            g = ps[0:NB, 1, :]
            step(v.tensor_scalar(g_sgn, g, 0.0, 2.0, ALU.is_ge, ALU.mult))
            step(v.tensor_scalar(g_sgn, g_sgn, -1.0, None, ALU.add))
            step(v.tensor_tensor(g_abs, g, g_sgn, ALU.mult))
            step(v.tensor_scalar(g_abs, g_abs, 0.25, None, ALU.max))
            step(v.tensor_tensor(g_abs, g_abs, g_sgn, ALU.mult))
            step(v.tensor_scalar(mrow[:, 0:D], g_abs[:, 0:D], 1.0 / WS, None, ALU.mult))
            step(v.tensor_tensor(mrow[:, D:2 * D], g_abs[:, 0:D], bo_bc, ALU.mult))
            step(v.tensor_copy(mrow[:, 2 * D:3 * D], g_abs[:, D:2 * D]))
            assert k[0] == ROWS_AT, k[0]
            for n in range(4):
                src = ps[:, 0, 2 * n * NB:2 * (n + 1) * NB].rearrange("p (c b) -> p c b", c=2)
                step(v.tensor_scalar(modT[:, :, 2 * n:2 * n + 2].rearrange("p b c -> p c b"), src, 1.0 if n % 2 == 0 else 0.0, None, ALU.add))
            for c in range(DC):
                split(moe_hi[:, c, :], moe_lo[:, c, :], ps[:, 6 + c, :])
            assert k[0] == SET_DVE, k[0]
            dve.wait_ge(s["set_ready"], 2)
            dve.wait_ge(s["rows_stored"], 16)

            def stats(b, xt, st, mv, ve, nm, loaded, names, norm, rs):
                wait(dve, *loaded)
                wait(dve, norm, b * QT)
                s_st, s_ag, s_rdy = names
                for t in range(QT):
                    v.bn_stats(st[:, t, :], xt[:, t, :]).then_inc(s[s_st], 1)
                wait(dve, s_st, (b + 1) * QT, "passed_dve")
                for t in range(QT):
                    v.bn_aggr(mv[:, t, :], st[:, t, :]).then_inc(s[s_ag], 1)
                wait(dve, s_ag, (b + 1) * QT)
                wait(dve, rs, b)
                v.tensor_scalar(ve[:], mv[:, :, 1], EPS, None, ALU.add).then_inc(s[s_rdy], 1)
                v.tensor_scalar(nm[:], mv[:, :, 0], -1.0, None, ALU.mult).then_inc(s[s_rdy], 1)

            def lo_part(b, n, hf_sem, hh_sem, hl_sem, hf, hh, hl, users):
                wait(dve, hh_sem, b * 2 + n + 1)
                for name, per in users:
                    wait(dve, name, b * per)
                v.tensor_tensor(hl[:, n, :], hf[:, n, :], hh[:, n, :], ALU.subtract).then_inc(s[hl_sem], 1)

            def side_step(name, n, b, bank):
                src = ps[:, MISC + bank, :]
                if name == "ta":
                    lo_part(b, n, "hfa_ready", "hha_ready", "hla_ready", hf_a, hh_a, hl_a,
                            [("v_ready", 2), ("qk_ready", 4)])
                elif name == "t2":
                    lo_part(b, n, "hfc_ready", "hhc_ready", "hlc_ready", hf_c, hh_c, hl_c, [("moe_ready", 4)])
                elif name == "qk":
                    wait(dve, "qk_hi", b * 4 + n + 1)
                    kk = n % 2
                    v.scalar_tensor_tensor(qk_st[:, kk, 1, :], src, bqk[:, 2 * kk + n // 2:2 * kk + n // 2 + 1],
                                           qk_st[:, kk, 0, :], ALU.add, ALU.subtract).then_inc(s["qk_lo"], 1)
                elif name == "out":
                    wait(dve, "out_ready", b * 2 + n + 1)
                    wait(dve, "ga_loaded", (b + 1) * 16)
                    wait(dve, "x1_ready", b * 2)
                    v.tensor_tensor(ot[:, 2 * n:2 * n + 2, :], src.rearrange("p (u d) -> p u d", u=2),
                                    ga_bc[:, 0:1, :].broadcast_to([P, 2, D]), ALU.mult).then_inc(s["ot_ready"], 1)
                elif name == "gate":
                    gates(b, src)
                elif name == "moe":
                    wait(dve, "z0_ready", b * 4 + n + 1)
                    wait(dve, "zg_ready", b * 2)
                    v.scalar_tensor_tensor(zs[:, n, :], ps[:, MISC + bank, D:2 * D], scl[:, 1, n:n + 1], z0[:, n, :],
                                           ALU.mult, ALU.add).then_inc(s["zs_ready"], 1)

            def gates(b, src):
                N = 8

                def did(m):
                    wait(dve, "gate_step", b * N + m)
                lg = src[:, 0:QT * E].rearrange("p (t e) -> p t e", t=QT)

                def bc(a):
                    return a[:].rearrange("p (t o) -> p t o", o=1).broadcast_to([P, QT, E])
                wait(dve, "gate_ready", b + 1)
                wait(dve, "zs_ready", b * 4)
                st = s["gate_step"]
                v.tensor_reduce(gmax[:], lg, AX.X, ALU.max).then_inc(st, 1)
                did(1)
                v.tensor_tensor(gsub[:], lg, bc(gmax), ALU.subtract).then_inc(st, 1)
                wait(dve, "gate_exp", b + 1)
                v.tensor_reduce(gsum[:], gexp[:], AX.X, ALU.add).then_inc(st, 1)
                did(3)
                v.reciprocal(grec[:], gsum[:]).then_inc(st, 1)
                did(4)
                v.tensor_tensor(gp[:], gexp[:], bc(grec), ALU.mult).then_inc(st, 1)
                did(5)
                v.tensor_scalar(gtop[:], gp[:], TOP_P, None, ALU.is_gt).then_inc(st, 1)
                did(6)
                v.tensor_reduce(gcnt[:], gtop[:], AX.X, ALU.add).then_inc(st, 1)
                did(7)
                v.tensor_scalar(gcnt0[:], gcnt[:], -1.0 / WS, float(E) / WS, ALU.mult, ALU.add).then_inc(st, 1)
                did(8)
                v.tensor_tensor(scl[:, 0, :], gcnt0[:], gp[:, :, 0], ALU.mult)
                v.scalar_tensor_tensor(scl[:, 1, :], gcnt[:], 1.0 / WS, gp[:, :, 1], ALU.mult,
                                       ALU.mult).then_inc(s["scl_ready"], 1)

            def maxima(b, h, n):
                g, j = h // 4, h % 4
                if n == 0 and j == 0:
                    wait(dve, "mt_ready", b * 4 + g - 3)
                wait(dve, "mx_ready", b * 48 + 3 * h + n + 1)
                bank = MX + (3 * h + n) % 2
                col = 0
                for qt in MPART[n]:
                    w = (qt + 1) * P
                    x_ = v.tensor_reduce(mxt[:, g, qt, j:j + 1], ps[:, bank, col:col + w], AX.X, ALU.max)
                    col += w
                x_.then_inc(s["mx_read"], 1)

            def invert(b):
                wait(dve, "zc_loaded", (b + 1) * 16)
                wait(dve, "rz_stored", b * 16)
                v.reciprocal(zr[:], zc[:]).then_inc(s["zr_ready"], 1)

            def normalise(b):
                wait(dve, "oc_loaded", (b + 1) * 32)
                wait(dve, "rz_loaded", (b + 1) * 32)
                wait(dve, "ol_ready", b * 2)
                v.tensor_tensor(om[:], oc[:], rz[:], ALU.mult).then_inc(s["om_ready"], 1)

            def o_lo(b):
                wait(dve, "oh_ready", b * 2 + 2)
                wait(dve, "out_ready", b * 2)
                for c in range(DC):
                    v.scalar_tensor_tensor(ol[:, c, :], om[:, c, :], bv[:, c:c + 1], oh[:, c, :], ALU.add,
                                           ALU.subtract).then_inc(s["ol_ready"], 1)

            def other(i, t):
                if t == 1 and live(i - 2):
                    stats(i - 2, x1, st_c, mv_c, ve_c, nm_c, ("x1_ready", (i - 2 + 1) * 2),
                          ("lnc_stats", "lnc_aggr", "lnc_ready"), "xnc_ready", "rsc_ready")
                if t == 12 and live(i + 2):
                    stats(i + 2, xa, st_a, mv_a, ve_a, nm_a, ("xa_loaded", (i + 2 + 1) * 16),
                          ("lna_stats", "lna_aggr", "lna_ready"), "xna_ready", "rsa_ready")
                if t == 7 and live(i - 1):
                    invert(i - 1)
                if t == 10 and live(i - 1):
                    normalise(i - 1)
                if t == 11 and live(i - 1):
                    o_lo(i - 1)

            def one(i):
                for t in range(SLOTS):
                    bm, hm = max_at(i, t)
                    for what in DVE_ORDER:
                        if what in "abc" and live(bm):
                            maxima(bm, hm, "abc".index(what))
                        if what == "s":
                            for name, n, b, bank in side(i, t):
                                side_step(name, n, b, bank)
                        if what == "S":
                            for name, n, b, bank in side(*((i, t - 1) if t else (i - 1, SLOTS - 1))):
                                side_step(name, n, b, bank)
                        if what == "o":
                            other(i, t)

            iterations(dve, one)

        @block.gpsimd
        def _(pool):
            q = nc.gpsimd
            q.memset(kz[:], 0.0).then_inc(s["set_ready"], 1)
            q.memset(qs[:], 0.0)
            q.memset(va[:], 1.0)
            q.memset(neg_half[:], -0.5)
            q.memset(zrow[:], 0.0).then_inc(s["set_ready"], 1)
            pool.wait_ge(s["set_ready"], 2)
            pool.wait_ge(s["rows_stored"], 16)
            wait(pool, "set_dve", SET_DVE, "passed_pool")
            wait(pool, "set_pe", SET_PE, "passed_pool")

            def norm(b, xt, xn, ve, nm, rs, ready, rs_sem, xn_sem, turned_sem):
                wait(pool, ready, (b + 1) * 2, "passed_pool")
                q.tensor_tensor(rs[:], ve[:], neg_half[:], ALU.pow).then_inc(s[rs_sem], 1)
                wait(pool, rs_sem, b + 1, "passed_pool")
                wait(pool, turned_sem, b * 2, "passed_pool")
                for t in range(QT):
                    q.tensor_scalar(xn[:, t, :], xt[:, t, :], nm[:, t:t + 1], rs[:, t:t + 1], ALU.add,
                                    ALU.mult).then_inc(s[xn_sem], 1)

            def spread(b, g):
                wait(pool, "v_evicted", (b + 1) * 2, "passed_pool")
                wait(pool, "pv_done", b * 16 - 4 * (3 - g), "passed_pool")
                q.tensor_scalar(va[:, :, 4 * g:4 * g + 4, 0:HD],
                                vst[:, :, 64 * g:64 * g + 64].rearrange("p t (h d) -> p t h d", h=4),
                                1.0, 0.0, ALU.mult, ALU.add).then_inc(s["va_ready"], 1)

            def add_bias(b):
                wait(pool, "xc_loaded", (b + 1) * 16, "passed_pool")
                wait(pool, "ga_loaded", (b + 1) * 16, "passed_pool")
                wait(pool, "x1_ready", b * 2, "passed_pool")
                q.tensor_tensor(xg[:], xc[:], ga_bc[:, 1:2, :].broadcast_to([P, QT, D]), ALU.add).then_inc(s["xg_ready"], 1)

            def residual(b, n):
                wait(pool, "ot_ready", b * 2 + n + 1, "passed_pool")
                wait(pool, "xg_ready", b + 1, "passed_pool")
                wait(pool, "lnc_stats", b * QT, "passed_pool")
                wait(pool, "xnc_ready", b * QT, "passed_pool")
                wait(pool, "res_ready", b * 2, "passed_pool")
                q.tensor_tensor(x1[:, 2 * n:2 * n + 2, :], ot[:, 2 * n:2 * n + 2, :], xg[:, 2 * n:2 * n + 2, :],
                                ALU.add).then_inc(s["x1_ready"], 1)

            def finish(b, n):
                wait(pool, "zs_ready", b * 4 + 2 * n + 2, "passed_pool")
                wait(pool, "gb_loaded", (b + 1) * 16, "passed_pool")
                wait(pool, "res_ready", b * 2, "passed_pool")
                t = slice(2 * n, 2 * n + 2)
                q.tensor_tensor(zg[:, t, :], zs[:, t, :], gb_bc[:].rearrange("p (o d) -> p o d", o=1).broadcast_to([P, 2, D]),
                                ALU.mult).then_inc(s["zg_ready"], 1)
                wait(pool, "zg_ready", b * 2 + n + 1, "passed_pool")
                wait(pool, "res_stored", b * 16, "passed_pool")
                q.tensor_tensor(res[:, t, :], zg[:, t, :], x1[:, t, :], ALU.add).then_inc(s["res_ready"], 1)

            def mask(b, h):
                wait(pool, "exp_done", b * 48 + 3 * h + 1, "passed_pool")
                d = prob[:, h % 8, 0:4 * P].rearrange("p (a t) -> p a t", a=4)
                q.affine_select(out=d, in_=d, compare_op=ALU.is_ge, fill=0.0, base=0, pattern=[[0, 4], [1, P]],
                                channel_multiplier=-1).then_inc(s["masked"], 1)

            def one(i):
                for t in range(SLOTS):
                    if live(i):
                        mask(i, t)
                    if t == 1 and live(i - 2):
                        norm(i - 2, x1, xn_c, ve_c, nm_c, rs_c, "lnc_ready", "rsc_ready", "xnc_ready", "t2_ready")
                    if t == 0 and live(i):
                        for g in range(3):
                            spread(i, g)
                    if t == 4 and live(i):
                        spread(i, 3)
                    if t == 9 and live(i - 1):
                        add_bias(i - 1)
                    if t == 12 and live(i - 2):
                        finish(i - 2, 0)
                    if t == 13 and live(i + 2):
                        norm(i + 2, xa, xn_a, ve_a, nm_a, rs_a, "lna_ready", "rsa_ready", "xna_ready", "ta_ready")
                    if t == 14 and live(i - 2):
                        finish(i - 2, 1)
                    if t == 15 and live(i - 1):
                        residual(i - 1, 0)
                        residual(i - 1, 1)

            iterations(pool, one)


_INS = ["L0_attn_x", "L0_attn_w_qkv", "L0_attn_b_qkv", "L0_attn_w_out", "L0_attn_b_out", "L0_ffn_gate_W",
        "L0_ffn_expert_W", "L0_ffn_out_W", "L0_c", "L0_wmod"]


def constants():
    at = np.arange(P)
    qk = np.where(at[None, :] > at[:, None], -1e30, 0.0).astype(np.float32)
    kaug = np.zeros((AUG, 16, 512), np.float16)
    kaug[0] = np.arange(512) * (FS / QONE)
    kaug[1, 0::2] = FS
    kaug[2, 1::2] = FS
    qaug = np.zeros((AUG, 8, 512), np.float16)
    qaug[0] = QONE
    for r in range(1, AUG - 2):
        kaug[2 + r, :, 32 * r:32 * r + 32] = FS
        qaug[2 + r, :, 0:32 * r] = -60000.0
    return {"ident": np.eye(P, dtype=np.float32), "mask_qk": qk, "kaug": kaug, "qaug": qaug}


def kernel(**inputs):
    import concourse.bacc as bacc
    from concourse.bass_utils import run_bass_kernel_spmd

    nc = bacc.Bacc("TRN2", target_bir_lowering=False, num_devices=1)
    arrays = {name: np.ascontiguousarray(inputs[name]) for name in _INS}
    arrays.update(constants())
    args = [nc.dram_tensor(f"in_{name}", a.shape, mybir.dt.from_np(a.dtype), kind="ExternalInput").ap()
            for name, a in arrays.items()]
    shape = arrays["L0_attn_x"].shape
    out = nc.dram_tensor("out_0", shape, F32, kind="ExternalOutput").ap()
    build(nc, *args, out)
    r = run_bass_kernel_spmd(nc, [{f"in_{name}": a for name, a in arrays.items()}], core_ids=[0])
    return r.results[0]["out_0"]
```

```python
from contextlib import ExitStack

import numpy as np

import concourse.bass as bass
from concourse import mybir

F32 = mybir.dt.float32
F16 = mybir.dt.float16
BF16 = mybir.dt.bfloat16
ALU = mybir.AluOpType
ACT = mybir.ActivationFunctionType
AX = mybir.AxisListType

P = 128
WS = 16.0
FS = 4 * WS * WS
QONE = 64.0
EPS = 1e-5
TOP_P = 0.3
SLOTS = 16
PE_ORDER = "01asub2wc"
ACT_ORDER = "o01su2"
DVE_ORDER = "SUaboc"
SIDE = {
    0: [("ta", 0, 1, 1), ("ta", 1, 1, 0)],
    1: [("mt", 1, 0, 1)],
    2: [("qk", 0, 1, 1)],
    3: [("qk", 1, 1, 0)],
    4: [("t2", 0, -2, 1), ("t2", 1, -2, 0)],
    5: [("mt", 2, 0, 1)],
    6: [("gate", 0, -2, 0)],
    7: [("qk", 2, 1, 1), ("v", 0, 1, 0)],
    8: [("moe", 0, -2, 0)],
    9: [("mt", 3, 0, 1), ("qk", 3, 1, 0)],
    10: [("moe", 1, -2, 1)],
    11: [("moe", 2, -2, 0)],
    12: [("moe", 3, -2, 1)],
    13: [("mt", 0, 1, 0)],
    14: [("out", 0, -1, 1)],
    15: [("v", 1, 1, 1), ("out", 1, -1, 0)],
}
SP_AT = {
    0: [("load_gb", None, -2)],
    2: [("load_aug", 1, 0), ("load_c", None, -1), ("load_a", None, 2), ("store_qk", 0, 1), ("store_qk", 1, 1)],
    3: [("store_ou", 2, -1), ("store_ou", 3, -1)],
    5: [("load_o", None, -1)],
    6: [("load_aug", 2, 0), ("load_stack", 0, 1), ("load_ga", None, -1)],
    8: [("load_stack", 1, 1), ("store_rz", None, -1), ("load_rz", None, -1), ("store_ou", 0, 0)],
    9: [("load_aug", 3, 0), ("store_qk", 3, 1)],
    11: [("load_modc", None, -1), ("store_ou", 1, 0), ("store_qk", 2, 1)],
    12: [("load_aug", 0, 1), ("load_stack", 2, 1)],
    14: [("load_stack", 3, 1)],
    15: [("store_res", None, -2)],
}
DVE_AT = {
    0: [("stats_c", 0, -2)],
    1: [("stats_c", 1, -2), ("aggregate_c", None, -2)],
    6: [("invert", None, -1)],
    11: [("o_lo", None, -1)],
    12: [("stats_a", 0, 2), ("stats_a", 1, 2)],
    13: [("aggregate_a", None, 2)],
}
POOL_AT = {
    1: [("spread", 2, 0)],
    2: [("spread", 0, 0)],
    3: [("spread", 1, 0), ("spread", 3, 0)],
    7: [("add_bias", None, -1)],
    9: [("normalise", None, -1)],
    10: [("finish", 0, -2)],
    13: [("norm_a", None, 2)],
    14: [("finish", 1, -2)],
    15: [("residual", 0, -1), ("residual", 1, -1), ("norm_c", None, -1)],
}
ACT_AT = {
    0: [("sums_out", 2, -1)],
    4: [("sums_out", 3, -1)],
    7: [("gate_exp", None, -2)],
    8: [("sums_out", 0, 0)],
    11: [("o_hi", None, -1)],
    12: [("sums_out", 1, 0)],
}
C_LOADS, M_LOADS, W_LOADS = 2, 2, 9
SILU, SILU_T, MOD, ROWS, OW_T, WEIGHTS, MOE = 3, 5, 9, 17, 18, 28, 32
PE_SILU_T, PE_MOD, PE_TURNED, PE_MOE = 1, 2, 3, 4
PARTS = 96
CONST = 112
STACK = 114
STACK_DMAS = 3


def build(nc, x, w_qkv, b_qkv, w_out, b_out, gate_w, expert_w, out_w, cond, wmod,
          ident_d, mask_qk_d, kaug_d, qaug_d, out):
    NB, S, D = x.shape
    H, HD = 16, 16
    QT = S // P
    DC = D // P
    E = gate_w.shape[0]
    HP = H // 2
    assert (S, D, QT, DC) == (512, 256, 4, 2) and E == 8

    ctx = ExitStack()
    with ctx:
        def sb(name, shape, dt):
            return ctx.enter_context(nc.sbuf_tensor(name, shape, dt))

        def sem(name):
            return ctx.enter_context(nc.semaphore(name))

        def dram(name, shape, dt):
            return nc.dram_tensor(name, shape, dt, kind="Internal").ap()

        ps = ctx.enter_context(nc.psum_tensor("ps", [P, 8, 512], F32))
        ST, MX, PVB, MISC = 0, 3, 5, 6

        ident = sb("ident", [P, P], F32)
        mask_qk = sb("mask_qk", [P, S], F32)
        wqkv_hi = sb("wqkv_hi", [P, DC, 3 * D], F16)
        wqkv_lo = sb("wqkv_lo", [P, DC, 3 * D], F16)
        wo_hi = sb("wo_hi", [P, DC, D], F16)
        wo_lo = sb("wo_lo", [P, DC, D], F16)
        moe_hi = sb("moe_hi", [P, DC, 2 * D], F16)
        moe_lo = sb("moe_lo", [P, DC, 2 * D], F16)
        gw_hi = sb("gw_hi", [P, DC, E], F16)
        gw_lo = sb("gw_lo", [P, DC, E], F16)
        bqk = sb("bqk", [P, 4], F32)
        bv = sb("bv", [P, DC], F32)
        modT = sb("modT", [P, NB, 8], F32)

        qs = sb("qs", [P, HP, S], F16)
        kz = sb("kz", [P, H, S], F16)
        prob = sb("prob", [P, 8, 10 * P], F32)
        va = sb("va", [P, QT, H, 32], F32)
        vst = sb("vst", [P, QT, D], F32)
        mxt = sb("mxt", [P, 4, QT, 4], F32)
        negm = sb("negm", [4, S], F16)
        xa = sb("xa", [P, QT, D], F32)
        xn_a = sb("xn_a", [P, QT, D], F32)
        mod_a = sb("mod_a", [P, 4], F32)
        st_a = sb("st_a", [P, QT, 6], F32)
        mv_a = sb("mv_a", [P, QT, 2], F32)
        ve_a = sb("ve_a", [P, QT], F32)
        nm_a = sb("nm_a", [P, QT], F32)
        rs_a = sb("rs_a", [P, QT], F32)
        hf_a = sb("hf_a", [P, DC, S], F32)
        hh_a = sb("hh_a", [P, DC, S], F16)
        hl_a = sb("hl_a", [P, DC, S], F16)
        qk_st = sb("qk_st", [P, 2, 2, S], F16)
        ou = sb("ou", [P, 4, S], F32)
        oc = sb("oc", [P, DC, S], F32)
        zc = sb("zc", [64, P], F32)
        zr = sb("zr", [64, P], F32)
        rz = sb("rz", [P, DC, S], F32)
        om = sb("om", [P, DC, S], F32)
        oh = sb("oh", [P, DC, S], F16)
        ol = sb("ol", [P, DC, S], F16)
        xc = sb("xc", [P, QT, D], F32)
        xg = sb("xg", [P, QT, D], F32)
        ga_bc = sb("ga_bc", [P, 2, D], F32)
        gb_bc = sb("gb_bc", [P, D], F32)
        ot = sb("ot", [P, QT, D], F32)
        x1 = sb("x1", [P, QT, D], F32)
        xn_c = sb("xn_c", [P, QT, D], F32)
        mod_c = sb("mod_c", [P, 4], F32)
        st_c = sb("st_c", [P, QT, 6], F32)
        mv_c = sb("mv_c", [P, QT, 2], F32)
        ve_c = sb("ve_c", [P, QT], F32)
        nm_c = sb("nm_c", [P, QT], F32)
        rs_c = sb("rs_c", [P, QT], F32)
        hf_c = sb("hf_c", [P, DC, S], F32)
        hh_c = sb("hh_c", [P, DC, S], F16)
        hl_c = sb("hl_c", [P, DC, S], F16)
        gmax = sb("gmax", [P, QT], F32)
        gsub = sb("gsub", [P, QT, E], F32)
        gexp = sb("gexp", [P, QT, E], F32)
        gsum = sb("gsum", [P, QT], F32)
        grec = sb("grec", [P, QT], F32)
        gp = sb("gp", [P, QT, E], F32)
        gtop = sb("gtop", [P, QT, E], F32)
        gcnt = sb("gcnt", [P, QT], F32)
        gcnt0 = sb("gcnt0", [P, QT], F32)
        scl = sb("scl", [P, 2, QT], F32)
        z0 = sb("z0", [P, QT, D], F32)
        zs = sb("zs", [P, QT, D], F32)
        zg = sb("zg", [P, QT, D], F32)
        res = sb("res", [P, QT, D], F32)
        neg_half = sb("neg_half", [P, QT], F32)

        spare = prob[:].rearrange("p a b -> p (a b)")
        taken = [0]

        def lend(rows, *dims):
            size = int(np.prod(dims))
            got = spare[0:rows, taken[0]:taken[0] + size]
            taken[0] += size
            if len(dims) == 2:
                got = got.rearrange("p (a b) -> p a b", a=dims[0])
            if len(dims) == 3:
                got = got.rearrange("p (a b c) -> p a b c", a=dims[0], b=dims[1])
            return got

        wq_nat, wo_nat, ow_nat = lend(P, 6, D), lend(P, DC, D), lend(P, DC, D)
        ex_nat, g_nat, c_nat = lend(P, 2, DC, D), lend(E, D), lend(NB, D)
        wm_nat, b_raw, bo_bc = lend(P, DC, 6 * D), lend(P, 4), lend(NB, D)
        c_exp, c_silu, c_silu_t = lend(NB, D), lend(NB, D), lend(P, DC, NB)
        g_sgn, g_abs, mrow = lend(NB, 2 * D), lend(NB, 2 * D), lend(NB, 3 * D)
        m_nat = lend(P, P)
        ow_t = vst[:, 0:2, :]

        qk_d = dram("qk_d", [2, 2, P, 3, S], F16)
        ou_d = dram("ou_d", [4 * P, S], F32)
        rz_d = dram("rz_d", [H, S], F32)
        rows_d = dram("rows_d", [NB, 3 * D], F32)

        block = ctx.enter_context(nc.Block())
        s = {}

        def sm(name):
            if name not in s:
                s[name] = sem(name)
            return s[name]

        for name in ("ld_c", "ld_m", "ld_w", "set_dve", "set_pe", "set_act", "set_ready", "rows_stored", "kaug_loaded",
                     "xa_loaded", "moda_loaded", "lna_stats", "lna_aggr", "lna_ready", "rsa_ready", "xna_ready",
                     "ta_ready", "hfa_ready", "hha_ready", "hla_ready", "qk_ready", "qk_hi", "qk_lo",
                     "qk_stored0", "qk_stored1", "qk_stored2", "qk_stored3", "stack_loaded0", "stack_loaded1",
                     "stack_loaded2", "stack_loaded3", "masked",
                     "v_ready", "v_evicted", "va_ready", "mx_ready", "mx_read", "mt_ready", "nm_ready",
                     "aug_loaded", "st_ready", "exp_done", "pv_done", "ou_ready", "ou_stored",
                     "zc_loaded", "oc_loaded", "zr_ready", "rz_stored", "rz_loaded", "om_ready", "oh_ready",
                     "ol_ready", "out_ready", "ot_ready", "x1_ready", "xc_loaded", "ga_loaded", "xg_ready",
                     "lnc_stats", "lnc_aggr", "lnc_ready", "rsc_ready", "xnc_ready", "modc_loaded", "gb_loaded",
                     "t2_ready", "hfc_ready", "hhc_ready", "hlc_ready", "gate_ready", "gate_step", "gate_exp",
                     "scl_ready", "moe_ready", "z0_ready", "zs_ready", "zg_ready", "res_ready", "res_stored",
                     "passed_sp", "passed_dve", "passed_pool"):
            sm(name)

        def wait(eng, name, value, passed=None):
            if isinstance(value, int) and value <= 0:
                return
            eng.wait_ge(s[name], value)
            if passed and not isinstance(value, int):
                eng.sem_inc(s[passed], 1)

        READ = {"ta": ("hha_ready", 2), "qk": ("qk_lo", 4), "mt": ("nm_ready", 4), "t2": ("hhc_ready", 2),
                "gate": ("gate_step", 8), "moe": ("zs_ready", 4), "v": ("v_evicted", 2), "out": ("ot_ready", 2)}

        def live(b):
            return not isinstance(b, int) or 0 <= b < NB

        def iterations(eng, one, first=-2):
            for i in range(first, 2):
                one(i)
            with eng.Fori(2, NB - 2) as i:
                one(i)
            for i in range(NB - 2, NB + 2):
                one(i)

        def side(i, t, pos):
            for name, n, off, bank in SIDE.get(t, [])[pos:pos + 1]:
                if live(i + off):
                    yield name, n, i + off, bank

        def before(i, t, pos, bank):
            order = [(u, q, st) for u in sorted(SIDE) for q, st in enumerate(SIDE[u])]
            at = [n for n, (u, q, _) in enumerate(order) if (u, q) == (t, pos)][0]
            for back in range(1, 3 * len(order)):
                laps, n = divmod(at - back, len(order))
                name, idx, off, bk = order[n][2]
                if bk == bank and live(i + off + laps):
                    return name, idx, i + off + laps
            return None

        def do(steps, table, i, t):
            for name, n, off in table.get(t, []):
                early = name in ("load_a", "stats_a", "aggregate_a", "norm_a")
                if live(i + off) and not (early and isinstance(i, int) and i + off == 0):
                    steps[name](*([i + off] if n is None else [i + off, n]))

        def max_at(i, t):
            return (i + 1, t - 8) if t >= 8 else (i, t + 8)

        CHUNK = [[(0, 0, 1), (1, 1, 1), (2, 2, 1), (3, 3, 1)], [(0, 1, 3), (2, 3, 1)], [(1, 2, 2)]]
        PCOL = {0: 4 * P, 1: 8 * P, 2: 7 * P}
        MPART = [[3], [2, 0], [1]]

        @block.sync
        def _(sp):
            def ld(name, dst, src, **kw):
                sp.dma_start(dst, src, **kw).then_inc(s[name], 16)
            ld("ld_c", c_nat, cond)
            ld("ld_c", ident[:], ident_d)
            sp.dma_start(xa[:], x[0].rearrange("(t p) d -> p t d", p=P)).then_inc(s["xa_loaded"], 16)
            ld("ld_m", wm_nat, wmod.rearrange("(k p) n -> p k n", p=P))
            ld("ld_m", bo_bc, b_out.rearrange("(o d) -> o d", o=1).broadcast_to([NB, D]))
            ld("ld_w", wq_nat, w_qkv.rearrange("(k p) d -> p k d", p=P))
            ld("ld_w", wo_nat, w_out.rearrange("(k p) d -> p k d", p=P))
            ld("ld_w", ow_nat, out_w.rearrange("(k p) d -> p k d", p=P))
            for e in range(2):
                ld("ld_w", ex_nat[:, e], expert_w[e].rearrange("(k p) d -> p k d", p=P))
            ld("ld_w", g_nat, gate_w)
            ld("ld_w", m_nat, mask_qk_d)
            ld("ld_w", b_raw, b_qkv[0:2 * D].rearrange("(c p) -> p c", p=P), allow_slow_non_contiguous=True)
            ld("ld_w", bv[:], b_qkv[2 * D:3 * D].rearrange("(c p) -> p c", p=P), allow_slow_non_contiguous=True)
            sp.wait_ge(s["set_ready"], 1)
            sp.dma_start(kz[PARTS:STACK, :, :], kaug_d).then_inc(s["kaug_loaded"], 16)
            sp.dma_start(qs[PARTS:STACK, :, :], qaug_d).then_inc(s["kaug_loaded"], 16)
            wait(sp, "set_dve", MOD, "passed_sp")
            sp.dma_start(mod_a[:], modT[:, 0, 0:4]).then_inc(s["moda_loaded"], 16)
            wait(sp, "set_dve", ROWS, "passed_sp")
            sp.dma_start(rows_d, mrow).then_inc(s["rows_stored"], 16)
            sp.wait_ge(s["rows_stored"], 16)
            sp.wait_ge(s["kaug_loaded"], 32)

            def load_a(b):
                wait(sp, "xna_ready", b * QT, "passed_sp")
                sp.dma_start(xa[:], x[b].rearrange("(t p) d -> p t d", p=P)).then_inc(s["xa_loaded"], 16)
                wait(sp, "hha_ready", b * 2, "passed_sp")
                sp.dma_start(mod_a[:], modT[:, b, 0:4]).then_inc(s["moda_loaded"], 16)

            def store_qk(b, n):
                wait(sp, "qk_lo", b * 4 + n + 1, "passed_sp")
                for g in (n // 2 * 2, n // 2 * 2 + 1):
                    wait(sp, f"stack_loaded{g}", b * STACK_DMAS * 16, "passed_sp")
                both = 1 - n % 2
                sp.dma_start(qk_d[n % 2, n // 2, :, both:both + 2, :], qk_st[:, n % 2]).then_inc(
                    s[f"qk_stored{n}"], 16)
                sp.dma_start(qk_d[n % 2, n // 2, :, 2 * (n % 2), :], qk_st[:, n % 2, 0]).then_inc(s[f"qk_stored{n}"], 16)

            def load_stack(b, g):
                c, at = g // 2, 64 * (g % 2)
                wait(sp, f"qk_stored{2 * c}", (b + 1) * 32, "passed_sp")
                wait(sp, f"qk_stored{2 * c + 1}", (b + 1) * 32, "passed_sp")
                wait(sp, "st_ready", b * 48 - 48 + 12 * (g + 1), "passed_sp")
                done = s[f"stack_loaded{g}"]
                pr = slice(2 * g, 2 * g + 2)
                src = qk_d[:, c, at:at + 64].rearrange("k (a j r) l t -> k a j (r l) t", a=2, j=2)
                sp.dma_start(qs[0:PARTS, pr, :], src[0].rearrange("a j r t -> (j r) a t")).then_inc(done, 16)
                for j in range(2):
                    sp.dma_start(kz[48 * j:48 * j + 48, 4 * g + j:4 * g + 4:2, :],
                                 src[1, :, j].rearrange("a r t -> r a t")).then_inc(done, 16)

            def load_aug(b, g):
                wait(sp, "nm_ready", b * 4 + g + 1, "passed_sp")
                for a in range(2):
                    sp.dma_start(qs[CONST:STACK, 2 * g + a, :], negm[2 * a:2 * a + 2, :]).then_inc(s["aug_loaded"], 16)

            def store_ou(b, g):
                wait(sp, "ou_ready", b * 4 + g + 1, "passed_sp")
                wait(sp, "oc_loaded", b * 32, "passed_sp")
                wait(sp, "zc_loaded", b * 16, "passed_sp")
                sp.dma_start(ou_d[P * g:P * (g + 1), :], ou[:, g, :]).then_inc(s["ou_stored"], 16)

            def load_o(b):
                wait(sp, "ou_stored", (b + 1) * 64, "passed_sp")
                wait(sp, "zr_ready", b, "passed_sp")
                sp.dma_start(zc[:], ou_d.rearrange("(h r) (u t) -> h r u t", r=32, u=4)[:, 16]).then_inc(
                    s["zc_loaded"], 16)
                wait(sp, "om_ready", b, "passed_sp")
                for c in range(DC):
                    src = ou_d.rearrange("(c h r) t -> c h r t", c=DC, r=32)[c, :, 0:HD, :]
                    sp.dma_start(oc[:, c, :], src).then_inc(s["oc_loaded"], 16)

            def store_rz(b):
                wait(sp, "zr_ready", b + 1, "passed_sp")
                wait(sp, "rz_loaded", b * 32, "passed_sp")
                sp.dma_start(rz_d.rearrange("h (u t) -> (h u) t", u=4), zr[:]).then_inc(s["rz_stored"], 16)

            def load_rz(b):
                wait(sp, "rz_stored", (b + 1) * 16, "passed_sp")
                for c in range(DC):
                    src = rz_d[8 * c:8 * c + 8, :].rearrange("h (o t) -> h o t", o=1).broadcast_to([8, HD, S])
                    sp.dma_start(rz[:, c, :], src).then_inc(s["rz_loaded"], 16)

            def load_c(b):
                wait(sp, "xg_ready", b, "passed_sp")
                sp.dma_start(xc[:], x[b].rearrange("(t p) d -> p t d", p=P)).then_inc(s["xc_loaded"], 16)

            def load_ga(b):
                wait(sp, "ot_ready", b * 2, "passed_sp")
                src = rows_d[bass.ds(b, 1), 0:2 * D].rearrange("o (k d) -> o k d", k=2).broadcast_to([P, 2, D])
                sp.dma_start(ga_bc[:], src).then_inc(s["ga_loaded"], 16)

            def load_gb(b):
                wait(sp, "zg_ready", b * 2, "passed_sp")
                sp.dma_start(gb_bc[:], rows_d[bass.ds(b, 1), 2 * D:3 * D].broadcast_to([P, D])).then_inc(
                    s["gb_loaded"], 16)

            def load_modc(b):
                wait(sp, "hhc_ready", b * 2, "passed_sp")
                sp.dma_start(mod_c[:], modT[:, b, 4:8]).then_inc(s["modc_loaded"], 16)

            def store_res(b):
                wait(sp, "res_ready", (b + 1) * 2, "passed_sp")
                sp.dma_start(out[b].rearrange("(t p) d -> p t d", p=P), res[:]).then_inc(s["res_stored"], 16)

            steps = dict(load_stack=load_stack, store_ou=store_ou, load_gb=load_gb, load_aug=load_aug, load_c=load_c,
                         store_qk=store_qk, load_a=load_a, load_o=load_o, load_ga=load_ga, store_rz=store_rz,
                         load_rz=load_rz, load_modc=load_modc, store_res=store_res)

            def one(i):
                for t in range(SLOTS):
                    do(steps, SP_AT, i, t)

            iterations(sp, one)
            wait(sp, "res_stored", NB * 16, "passed_sp")

        @block.tensor
        def _(pe):
            mm = nc.tensor.matmul

            def turn(n, src, rows=P):
                return nc.tensor.transpose(ps[:, n // 4, (n % 4) * P:(n % 4) * P + rows], src, ident[0:rows, 0:rows])

            pe.wait_ge(s["ld_c"], C_LOADS * 16)
            pe.wait_ge(s["set_dve"], SILU)
            for c in range(DC):
                x_ = turn(22 + c, c_silu[:, c * P:(c + 1) * P], NB)
            x_.then_inc(s["set_pe"], 1)
            pe.wait_ge(s["ld_m"], M_LOADS * 16)
            pe.wait_ge(s["set_dve"], SILU_T)
            for n, part in enumerate((1, 0, 4, 3)):
                for c in range(DC):
                    for k in range(DC):
                        col = part * D + c * P
                        mm(ps[:, 6, (2 * n + c) * NB:(2 * n + c + 1) * NB], wm_nat[:, k, col:col + P],
                           c_silu_t[:, k, :], start=(k == 0), stop=(k == DC - 1))
            for n, part in enumerate((2, 5)):
                for k in range(DC):
                    x_ = mm(ps[0:NB, 7, n * D:(n + 1) * D], c_silu_t[:, k, :],
                            wm_nat[:, k, part * D:(part + 1) * D], start=(k == 0), stop=(k == DC - 1))
            x_.then_inc(s["set_pe"], 1)
            pe.wait_ge(s["ld_w"], W_LOADS * 16)
            for c in range(DC):
                for k in range(6):
                    turn(c * 6 + k, wq_nat[:, k, c * P:(c + 1) * P])
                for k in range(DC):
                    turn(12 + c * 2 + k, wo_nat[:, k, c * P:(c + 1) * P])
                    turn(16 + c * 2 + k, ow_nat[:, k, c * P:(c + 1) * P])
            for c in range(DC):
                x_ = turn(20 + c, g_nat[:, c * P:(c + 1) * P], E)
            x_.then_inc(s["set_pe"], 1)
            pe.wait_ge(s["set_dve"], ROWS)
            pe.wait_ge(s["set_ready"], 3)
            pe.wait_ge(s["kaug_loaded"], 32)

            def experts():
                pe.wait_ge(s["set_dve"], WEIGHTS)
                for c in range(DC):
                    for e in range(2):
                        for k in range(DC):
                            x_ = mm(ps[:, ST + c, e * D:(e + 1) * D], ex_nat[:, e, k, c * P:(c + 1) * P],
                                    ow_t[:, k, :], start=(k == 0), stop=(k == DC - 1))
                x_.then_inc(s["set_pe"], 1)

            def products(dst, pairs):
                for n, (a, b) in enumerate(pairs):
                    x_ = mm(dst, a, b, start=(n == 0), stop=(n == len(pairs) - 1))
                return x_

            def side_step(name, n, b, bank, prev):
                if prev is not None:
                    pname, pn, pb = prev
                    rd, per = READ[pname]
                    wait(pe, rd, pb * per + (2 if pname == "gate" else pn + 1))
                dst = ps[:, MISC + bank, :]
                if name == "ta":
                    wait(pe, "xna_ready", (b + 1) * QT)
                    for t in range(QT):
                        x_ = nc.tensor.transpose(dst[:, t * P:(t + 1) * P], xn_a[:, t, n * P:(n + 1) * P], ident[:])
                    x_.then_inc(s["ta_ready"], 1)
                elif name == "t2":
                    wait(pe, "xnc_ready", (b + 1) * QT)
                    for t in range(QT):
                        x_ = nc.tensor.transpose(dst[:, t * P:(t + 1) * P], xn_c[:, t, n * P:(n + 1) * P], ident[:])
                    x_.then_inc(s["t2_ready"], 1)
                elif name == "qk":
                    wait(pe, "hla_ready", (b + 1) * 2)
                    col = (n % 2) * D + (n // 2) * P
                    w = slice(col, col + P)
                    pairs = []
                    for c in range(DC):
                        pairs += [(wqkv_hi[:, c, w], hh_a[:, c, :]), (wqkv_hi[:, c, w], hl_a[:, c, :]),
                                  (wqkv_lo[:, c, w], hh_a[:, c, :])]
                    products(dst, pairs).then_inc(s["qk_ready"], 1)
                elif name == "v":
                    for u in range(2):
                        t = slice((2 * n + u) * P, (2 * n + u + 1) * P)
                        pairs = []
                        for c in range(DC):
                            pairs += [(hh_a[:, c, t], wqkv_hi[:, c, 2 * D:]), (hh_a[:, c, t], wqkv_lo[:, c, 2 * D:]),
                                      (hl_a[:, c, t], wqkv_hi[:, c, 2 * D:])]
                        x_ = products(dst[:, u * D:(u + 1) * D], pairs)
                    x_.then_inc(s["v_ready"], 1)
                elif name == "mt":
                    wait(pe, "mx_read", b * 48 + 12 * (n + 1))
                    for t in range(QT):
                        x_ = nc.tensor.transpose(dst[0:4, t * P:(t + 1) * P], mxt[:, n, t, :], ident[:])
                    x_.then_inc(s["mt_ready"], 1)
                elif name == "out":
                    wait(pe, "ol_ready", (b + 1) * 2)
                    for u in range(2):
                        t = slice((2 * n + u) * P, (2 * n + u + 1) * P)
                        pairs = []
                        for c in range(DC):
                            pairs += [(oh[:, c, t], wo_hi[:, c, :]), (oh[:, c, t], wo_lo[:, c, :]),
                                      (ol[:, c, t], wo_hi[:, c, :])]
                        x_ = products(dst[:, u * D:(u + 1) * D], pairs)
                    x_.then_inc(s["out_ready"], 1)
                elif name == "gate":
                    wait(pe, "hlc_ready", (b + 1) * 2)
                    for u in range(QT):
                        t = slice(u * P, (u + 1) * P)
                        pairs = []
                        for c in range(DC):
                            pairs += [(hh_c[:, c, t], gw_hi[:, c, :]), (hh_c[:, c, t], gw_lo[:, c, :]),
                                      (hl_c[:, c, t], gw_hi[:, c, :])]
                        x_ = products(dst[:, u * E:(u + 1) * E], pairs)
                    x_.then_inc(s["gate_ready"], 1)
                elif name == "moe":
                    t = slice(n * P, (n + 1) * P)
                    pairs = []
                    for c in range(DC):
                        pairs += [(hh_c[:, c, t], moe_hi[:, c, :]), (hh_c[:, c, t], moe_lo[:, c, :]),
                                  (hl_c[:, c, t], moe_hi[:, c, :])]
                    products(dst, pairs).then_inc(s["moe_ready"], 1)

            def scores(b, h, n):
                if h % 4 == 0 and n == 0:
                    wait(pe, "aug_loaded", (b * 4 + h // 4 + 1) * 32)
                wait(pe, "exp_done", b * 48 + 3 * h + n - 2)
                col = 0
                for kt, qt, w in CHUNK[n]:
                    x_ = mm(ps[:, ST + n, col:col + w * P], kz[0:STACK, h, kt * P:(kt + 1) * P],
                            qs[0:STACK, h // 2, qt * P:(qt + w) * P], start=True, stop=True)
                    col += w * P
                x_.then_inc(s["st_ready"], 1)

            def row_scores(b, h, n):
                if h % 4 == 0 and n == 0:
                    wait(pe, f"stack_loaded{h // 4}", (b + 1) * STACK_DMAS * 16)
                wait(pe, "mx_read", b * 48 + 3 * h + n - 1)
                bank = MX + (3 * h + n) % 2
                col = 0
                for qt in MPART[n]:
                    w = (qt + 1) * P
                    x_ = mm(ps[:, bank, col:col + w], qs[0:CONST, h // 2, qt * P:(qt + 1) * P], kz[0:CONST, h, 0:w],
                            start=True, stop=True)
                    col += w
                x_.then_inc(s["mx_ready"], 1)

            def weigh(b, g, kt):
                if kt == 0:
                    wait(pe, "exp_done", b * 48 + 12 * (g + 1))
                    wait(pe, "masked", b * 16 + 4 * (g + 1))
                    wait(pe, "va_ready", b * 4 + g + 1)
                    wait(pe, "ou_ready", b * 4 + g)
                for j in range(4):
                    h = 4 * g + j
                    x_ = mm(ps[32 * j:32 * j + 32, PVB, kt * P:(kt + 1) * P], va[:, kt, h, :],
                            prob[:, h % 8, kt * P:(kt + 1) * P], start=(kt == 0), stop=(kt == QT - 1))
                if kt < QT - 1:
                    for j in range(4):
                        h = 4 * g + j
                        w = (QT - 1 - kt) * P
                        x_ = mm(ps[32 * j:32 * j + 32, PVB, (kt + 1) * P:S], va[:, kt, h, :],
                                prob[:, h % 8, PCOL[kt]:PCOL[kt] + w], start=False, stop=False)
                x_.then_inc(s["pv_done"], 1)

            def one(i):
                if isinstance(i, int) and i == 0:
                    pe.wait_ge(s["set_dve"], MOE)
                for t in range(SLOTS):
                    if isinstance(i, int) and (i, t) == (-1, 1):
                        experts()
                    bm, hm = max_at(i, t)
                    bp = i if t >= 4 else i - 1
                    for what in PE_ORDER:
                        if what in "012" and live(i):
                            scores(i, t, int(what))
                        if what in "abc" and live(bm):
                            row_scores(bm, hm, "abc".index(what))
                        if what in "su":
                            pos = "su".index(what)
                            for name, n, b, bank in side(i, t, pos):
                                side_step(name, n, b, bank, before(i, t, pos, bank))
                        if what == "w" and live(bp):
                            weigh(bp, (t // 4 - 1) % 4, t % 4)

            iterations(pe, one)

        @block.scalar
        def _(act):
            act.wait_ge(s["ld_c"], C_LOADS * 16)
            nc.scalar.activation(c_exp, c_nat, ACT.Exp, scale=-1.0).then_inc(s["set_act"], 1)
            act.wait_ge(s["set_ready"], 3)

            def exp(b, h, n):
                if n == 0 and h % 4 == 0:
                    wait(act, "pv_done", b * 16 + h - 4)
                wait(act, "st_ready", b * 48 + 3 * h + n + 1)
                at, w = [(0, 512), (512, 512), (1024, 256)][n]
                nc.scalar.activation(prob[:, h % 8, at:at + w], ps[:, ST + n, 0:w], ACT.Exp,
                                     scale=1.0 / FS).then_inc(s["exp_done"], 1)

            def turned(b, n, bank, ready, mod, loaded, hf, hh, hf_sem, hh_sem, hl_sem, users):
                wait(act, ready, b * 2 + n + 1)
                wait(act, loaded, (b + 1) * 16)
                wait(act, hl_sem, b * 2)
                for name, per in users:
                    wait(act, name, b * per)
                src = ps[:, MISC + bank, :]
                nc.scalar.activation(hf[:, n, :], src, ACT.Identity, bias=mod[:, 2 + n:3 + n],
                                     scale=mod[:, n:n + 1]).then_inc(s[hf_sem], 1)
                nc.scalar.activation(hh[:, n, :], src, ACT.Identity, bias=mod[:, 2 + n:3 + n],
                                     scale=mod[:, n:n + 1]).then_inc(s[hh_sem], 1)

            def side_step(name, n, b, bank):
                src = ps[:, MISC + bank, :]
                if name == "ta":
                    turned(b, n, bank, "ta_ready", mod_a, "moda_loaded", hf_a, hh_a, "hfa_ready", "hha_ready",
                           "hla_ready", [("v_ready", 2), ("qk_ready", 4)])
                elif name == "t2":
                    turned(b, n, bank, "t2_ready", mod_c, "modc_loaded", hf_c, hh_c, "hfc_ready", "hhc_ready",
                           "hlc_ready", [("moe_ready", 4)])
                elif name == "qk":
                    wait(act, "qk_ready", b * 4 + n + 1)
                    k = n % 2
                    if n >= 2:
                        wait(act, f"qk_stored{n - 2}", (b + 1) * 32)
                    else:
                        wait(act, f"qk_stored{n + 2}", b * 32)
                    nc.scalar.activation(qk_st[:, k, 0, :], src, ACT.Identity,
                                         bias=bqk[:, 2 * k + n // 2:2 * k + n // 2 + 1]).then_inc(s["qk_hi"], 1)
                elif name == "v":
                    wait(act, "v_ready", b * 2 + n + 1)
                    wait(act, "va_ready", b * 4)
                    nc.scalar.activation(vst[:, 2 * n:2 * n + 2, :], src.rearrange("p (u d) -> p u d", u=2),
                                         ACT.Copy, scale=1.0 / WS).then_inc(s["v_evicted"], 1)
                elif name == "mt":
                    wait(act, "mt_ready", b * 4 + n + 1)
                    wait(act, "aug_loaded", (b * 4 + n) * 32)
                    nc.scalar.activation(negm[:], ps[0:4, MISC + bank, :], ACT.Copy,
                                         scale=-1.0 / FS).then_inc(s["nm_ready"], 1)
                elif name == "moe":
                    wait(act, "moe_ready", b * 4 + n + 1)
                    wait(act, "scl_ready", b + 1)
                    wait(act, "zs_ready", b * 4)
                    nc.scalar.activation(z0[:, n, :], ps[:, MISC + bank, 0:D], ACT.Copy,
                                         scale=scl[:, 0, n:n + 1]).then_inc(s["z0_ready"], 1)

            def sums_out(b, g):
                wait(act, "pv_done", b * 16 + 4 * g + 4)
                if g == 0:
                    wait(act, "ou_stored", b * 64)
                nc.scalar.activation(ou[:, g, :], ps[:, PVB, :], ACT.Copy).then_inc(s["ou_ready"], 1)

            def gate_exp(b):
                wait(act, "gate_step", b * 8 + 2)
                wait(act, "gate_step", b * 8)
                nc.scalar.activation(gexp[:], gsub[:], ACT.Exp, scale=1.0 / WS).then_inc(s["gate_exp"], 1)

            def o_hi(b):
                wait(act, "om_ready", b + 1)
                wait(act, "out_ready", b * 2)
                wait(act, "ol_ready", b * 2)
                for c in range(DC):
                    nc.scalar.activation(oh[:, c, :], om[:, c, :], ACT.Identity,
                                         bias=bv[:, c:c + 1]).then_inc(s["oh_ready"], 1)

            def one(i):
                if isinstance(i, int) and i == 0:
                    act.wait_ge(s["set_dve"], MOE)
                    act.wait_ge(s["rows_stored"], 16)
                for t in range(SLOTS):
                    if isinstance(i, int) and (i, t) == (-1, 1):
                        act.wait_ge(s["set_dve"], WEIGHTS)
                        act.wait_ge(s["ld_w"], W_LOADS * 16)
                    for what in ACT_ORDER:
                        if what in "012" and live(i):
                            exp(i, t, int(what))
                        if what == "o":
                            do(steps, ACT_AT, i, t)
                        if what in "su":
                            for name, n, b, bank in side(i, t, "su".index(what)):
                                side_step(name, n, b, bank)
                        if what in "SU":
                            for name, n, b, bank in side(*((i, t - 1) if t else (i - 1, SLOTS - 1)), "SU".index(what)):
                                side_step(name, n, b, bank)

            steps = dict(sums_out=sums_out, gate_exp=gate_exp, o_hi=o_hi)
            iterations(act, one)

        @block.vector
        def _(dve):
            v = nc.vector
            k = [0]

            def step(ins):
                k[0] += 1
                ins.then_inc(s["set_dve"], 1)
                dve.wait_ge(s["set_dve"], k[0])

            def stats(xt, st, loaded, per, name, norm):
                def two(b, n):
                    wait(dve, loaded, (b + 1) * per)
                    wait(dve, norm, b * QT)
                    for t in (2 * n, 2 * n + 1):
                        v.bn_stats(st[:, t, :], xt[:, t, :]).then_inc(s[name], 1)
                return two

            def aggregate(st, mv, ve, nm, names, norm, rs):
                s_st, s_ag, s_rdy = names

                def whole(b):
                    wait(dve, norm, b * QT)
                    wait(dve, s_st, (b + 1) * QT, "passed_dve")
                    for t in range(QT):
                        v.bn_aggr(mv[:, t, :], st[:, t, :]).then_inc(s[s_ag], 1)
                    wait(dve, s_ag, (b + 1) * QT)
                    wait(dve, rs, b)
                    v.tensor_scalar(ve[:], mv[:, :, 1], EPS, None, ALU.add).then_inc(s[s_rdy], 1)
                    v.tensor_scalar(nm[:], mv[:, :, 0], -1.0, None, ALU.mult).then_inc(s[s_rdy], 1)
                return whole

            def lo_part(b, n, hf_sem, hh_sem, hl_sem, hf, hh, hl, users):
                wait(dve, hh_sem, b * 2 + n + 1)
                for name, per in users:
                    wait(dve, name, b * per)
                v.tensor_tensor(hl[:, n, :], hf[:, n, :], hh[:, n, :], ALU.subtract).then_inc(s[hl_sem], 1)

            def side_step(name, n, b, bank):
                src = ps[:, MISC + bank, :]
                if name == "ta":
                    lo_part(b, n, "hfa_ready", "hha_ready", "hla_ready", hf_a, hh_a, hl_a,
                            [("v_ready", 2), ("qk_ready", 4)])
                elif name == "t2":
                    lo_part(b, n, "hfc_ready", "hhc_ready", "hlc_ready", hf_c, hh_c, hl_c, [("moe_ready", 4)])
                elif name == "qk":
                    wait(dve, "qk_hi", b * 4 + n + 1)
                    kk = n % 2
                    v.scalar_tensor_tensor(qk_st[:, kk, 1, :], src, bqk[:, 2 * kk + n // 2:2 * kk + n // 2 + 1],
                                           qk_st[:, kk, 0, :], ALU.add, ALU.subtract).then_inc(s["qk_lo"], 1)
                elif name == "out":
                    wait(dve, "out_ready", b * 2 + n + 1)
                    wait(dve, "ga_loaded", (b + 1) * 16)
                    wait(dve, "x1_ready", b * 2)
                    v.tensor_tensor(ot[:, 2 * n:2 * n + 2, :], src.rearrange("p (u d) -> p u d", u=2),
                                    ga_bc[:, 0:1, :].broadcast_to([P, 2, D]), ALU.mult).then_inc(s["ot_ready"], 1)
                elif name == "gate":
                    gates(b, src)
                elif name == "moe":
                    wait(dve, "z0_ready", b * 4 + n + 1)
                    wait(dve, "zg_ready", b * 2)
                    v.scalar_tensor_tensor(zs[:, n, :], ps[:, MISC + bank, D:2 * D], scl[:, 1, n:n + 1], z0[:, n, :],
                                           ALU.mult, ALU.add).then_inc(s["zs_ready"], 1)

            def gates(b, src):
                N = 8

                def did(m):
                    wait(dve, "gate_step", b * N + m)
                lg = src[:, 0:QT * E].rearrange("p (t e) -> p t e", t=QT)

                def bc(a):
                    return a[:].rearrange("p (t o) -> p t o", o=1).broadcast_to([P, QT, E])
                wait(dve, "gate_ready", b + 1)
                wait(dve, "zs_ready", b * 4)
                st = s["gate_step"]
                v.tensor_reduce(gmax[:], lg, AX.X, ALU.max).then_inc(st, 1)
                did(1)
                v.tensor_tensor(gsub[:], lg, bc(gmax), ALU.subtract).then_inc(st, 1)
                wait(dve, "gate_exp", b + 1)
                v.tensor_reduce(gsum[:], gexp[:], AX.X, ALU.add).then_inc(st, 1)
                did(3)
                v.reciprocal(grec[:], gsum[:]).then_inc(st, 1)
                did(4)
                v.tensor_tensor(gp[:], gexp[:], bc(grec), ALU.mult).then_inc(st, 1)
                did(5)
                v.tensor_scalar(gtop[:], gp[:], TOP_P, None, ALU.is_gt).then_inc(st, 1)
                did(6)
                v.tensor_reduce(gcnt[:], gtop[:], AX.X, ALU.add).then_inc(st, 1)
                did(7)
                v.tensor_scalar(gcnt0[:], gcnt[:], -1.0 / WS, float(E) / WS, ALU.mult, ALU.add).then_inc(st, 1)
                did(8)
                v.tensor_tensor(scl[:, 0, :], gcnt0[:], gp[:, :, 0], ALU.mult)
                v.scalar_tensor_tensor(scl[:, 1, :], gcnt[:], 1.0 / WS, gp[:, :, 1], ALU.mult,
                                       ALU.mult).then_inc(s["scl_ready"], 1)

            def maxima(b, h, n):
                g, j = h // 4, h % 4
                if n == 0 and j == 0:
                    wait(dve, "mt_ready", b * 4 + g - 3)
                wait(dve, "mx_ready", b * 48 + 3 * h + n + 1, "passed_dve")
                bank = MX + (3 * h + n) % 2
                col = 0
                for qt in MPART[n]:
                    w = (qt + 1) * P
                    x_ = v.tensor_tensor_reduce(ps[:, bank, col:col + w], ps[:, bank, col:col + w], mask_qk[:, S - w:S],
                                                1.0, -3e38, ALU.add, ALU.max, mxt[:, g, qt, j:j + 1])
                    col += w
                x_.then_inc(s["mx_read"], 1)

            def invert(b):
                wait(dve, "zc_loaded", (b + 1) * 16)
                wait(dve, "rz_stored", b * 16)
                v.reciprocal(zr[:], zc[:]).then_inc(s["zr_ready"], 1)

            def o_lo(b):
                wait(dve, "om_ready", b + 1)
                wait(dve, "oh_ready", b * 2 + 2)
                wait(dve, "out_ready", b * 2)
                for c in range(DC):
                    v.scalar_tensor_tensor(ol[:, c, :], om[:, c, :], bv[:, c:c + 1], oh[:, c, :], ALU.add,
                                           ALU.subtract).then_inc(s["ol_ready"], 1)

            steps = dict(
                stats_a=stats(xa, st_a, "xa_loaded", 16, "lna_stats", "xna_ready"),
                stats_c=stats(x1, st_c, "x1_ready", 2, "lnc_stats", "xnc_ready"),
                aggregate_a=aggregate(st_a, mv_a, ve_a, nm_a, ("lna_stats", "lna_aggr", "lna_ready"), "xna_ready", "rsa_ready"),
                aggregate_c=aggregate(st_c, mv_c, ve_c, nm_c, ("lnc_stats", "lnc_aggr", "lnc_ready"), "xnc_ready", "rsc_ready"),
                invert=invert, o_lo=o_lo)

            dve.wait_ge(s["ld_c"], C_LOADS * 16)
            dve.wait_ge(s["set_act"], 1)
            step(v.tensor_scalar(c_exp, c_exp, 1.0, None, ALU.add))
            step(v.reciprocal(c_exp, c_exp))
            step(v.tensor_tensor(c_silu, c_exp, c_nat, ALU.mult))
            assert k[0] == SILU
            dve.wait_ge(s["set_pe"], PE_SILU_T)
            flat = ps[:].rearrange("p a b -> p (a b)")
            for c in range(DC):
                step(v.tensor_copy(c_silu_t[:, c, :], flat[:, (22 + c) * P:(22 + c) * P + NB]))
            assert k[0] == SILU_T
            for n in range(2):
                steps["stats_a"](0, n)
            steps["aggregate_a"](0)
            dve.wait_ge(s["set_pe"], PE_MOD)
            dve.wait_ge(s["ld_m"], M_LOADS * 16)
            for n in range(4):
                src = ps[:, 6, 2 * n * NB:2 * (n + 1) * NB].rearrange("p (c b) -> p c b", c=2)
                step(v.tensor_scalar(modT[:, :, 2 * n:2 * n + 2].rearrange("p b c -> p c b"), src,
                                     1.0 if n % 2 == 0 else 0.0, None, ALU.add))
            assert k[0] == MOD
            g = ps[0:NB, 7, :]
            step(v.tensor_scalar(g_sgn, g, 0.0, 2.0, ALU.is_ge, ALU.mult))
            step(v.tensor_scalar(g_sgn, g_sgn, -1.0, None, ALU.add))
            step(v.tensor_tensor(g_abs, g, g_sgn, ALU.mult))
            step(v.tensor_scalar(g_abs, g_abs, 0.25, None, ALU.max))
            step(v.tensor_tensor(g_abs, g_abs, g_sgn, ALU.mult))
            step(v.tensor_scalar(mrow[:, 0:D], g_abs[:, 0:D], 1.0 / WS, None, ALU.mult))
            step(v.tensor_tensor(mrow[:, D:2 * D], g_abs[:, 0:D], bo_bc, ALU.mult))
            step(v.tensor_copy(mrow[:, 2 * D:3 * D], g_abs[:, D:2 * D]))
            assert k[0] == ROWS

            def split(hi, lo, src):
                step(v.tensor_scalar(hi, src, WS, None, ALU.mult))
                step(v.scalar_tensor_tensor(lo, src, WS, hi, ALU.mult, ALU.subtract))

            dve.wait_ge(s["set_pe"], PE_TURNED)
            dve.wait_ge(s["ld_w"], W_LOADS * 16)
            step(v.tensor_copy(ow_t.rearrange("p c n -> p (c n)"), flat[:, 16 * P:20 * P]))
            assert k[0] == OW_T
            split(wqkv_hi[:].rearrange("p c n -> p (c n)"), wqkv_lo[:].rearrange("p c n -> p (c n)"),
                  flat[:, 0:12 * P])
            split(wo_hi[:].rearrange("p c n -> p (c n)"), wo_lo[:].rearrange("p c n -> p (c n)"),
                  flat[:, 12 * P:16 * P])
            for c in range(DC):
                split(gw_hi[:, c, :], gw_lo[:, c, :], flat[:, (20 + c) * P:(20 + c) * P + E])
            step(v.tensor_scalar(bqk[:], b_raw, WS, None, ALU.mult))
            step(v.tensor_copy(mask_qk[:, S - P:S], m_nat))
            assert k[0] == WEIGHTS
            dve.wait_ge(s["set_ready"], 3)

            def split_experts():
                dve.wait_ge(s["set_pe"], PE_MOE)
                for c in range(DC):
                    split(moe_hi[:, c, :], moe_lo[:, c, :], ps[:, ST + c, :])
                assert k[0] == MOE

            def one(i):
                for t in range(SLOTS):
                    if isinstance(i, int) and (i, t) == (-1, 7):
                        split_experts()
                    bm, hm = max_at(i, t)
                    for what in DVE_ORDER:
                        if what in "abc" and live(bm):
                            maxima(bm, hm, "abc".index(what))
                        if what in "su":
                            for name, n, b, bank in side(i, t, "su".index(what)):
                                side_step(name, n, b, bank)
                        if what in "SU":
                            for name, n, b, bank in side(*((i, t - 1) if t else (i - 1, SLOTS - 1)), "SU".index(what)):
                                side_step(name, n, b, bank)
                        if what == "o":
                            do(steps, DVE_AT, i, t)

            iterations(dve, one)

        @block.gpsimd
        def _(pool):
            q = nc.gpsimd
            def norm(b, xt, xn, ve, nm, rs, ready, rs_sem, xn_sem, turned_sem):
                wait(pool, ready, (b + 1) * 2, "passed_pool")
                q.tensor_tensor(rs[:], ve[:], neg_half[:], ALU.pow).then_inc(s[rs_sem], 1)
                wait(pool, rs_sem, b + 1, "passed_pool")
                wait(pool, turned_sem, b * 2, "passed_pool")
                for t in range(QT):
                    q.tensor_scalar(xn[:, t, :], xt[:, t, :], nm[:, t:t + 1], rs[:, t:t + 1], ALU.add,
                                    ALU.mult).then_inc(s[xn_sem], 1)

            def spread(b, g):
                wait(pool, "v_evicted", (b + 1) * 2, "passed_pool")
                wait(pool, "pv_done", b * 16 - 4 * (3 - g), "passed_pool")
                q.tensor_scalar(va[:, :, 4 * g:4 * g + 4, 0:HD],
                                vst[:, :, 64 * g:64 * g + 64].rearrange("p t (h d) -> p t h d", h=4),
                                1.0, 0.0, ALU.mult, ALU.add).then_inc(s["va_ready"], 1)

            def normalise(b):
                wait(pool, "oc_loaded", (b + 1) * 32, "passed_pool")
                wait(pool, "rz_loaded", (b + 1) * 32, "passed_pool")
                wait(pool, "oh_ready", b * 2, "passed_pool")
                wait(pool, "ol_ready", b * 2, "passed_pool")
                q.tensor_tensor(om[:], oc[:], rz[:], ALU.mult).then_inc(s["om_ready"], 1)

            def add_bias(b):
                wait(pool, "xc_loaded", (b + 1) * 16, "passed_pool")
                wait(pool, "ga_loaded", (b + 1) * 16, "passed_pool")
                wait(pool, "x1_ready", b * 2, "passed_pool")
                q.tensor_tensor(xg[:], xc[:], ga_bc[:, 1:2, :].broadcast_to([P, QT, D]), ALU.add).then_inc(s["xg_ready"], 1)

            def residual(b, n):
                wait(pool, "ot_ready", b * 2 + n + 1, "passed_pool")
                wait(pool, "xg_ready", b + 1, "passed_pool")
                wait(pool, "lnc_stats", b * QT, "passed_pool")
                wait(pool, "xnc_ready", b * QT, "passed_pool")
                wait(pool, "res_ready", b * 2, "passed_pool")
                q.tensor_tensor(x1[:, 2 * n:2 * n + 2, :], ot[:, 2 * n:2 * n + 2, :], xg[:, 2 * n:2 * n + 2, :],
                                ALU.add).then_inc(s["x1_ready"], 1)

            def finish(b, n):
                wait(pool, "zs_ready", b * 4 + 2 * n + 2, "passed_pool")
                wait(pool, "gb_loaded", (b + 1) * 16, "passed_pool")
                wait(pool, "res_ready", b * 2, "passed_pool")
                t = slice(2 * n, 2 * n + 2)
                q.tensor_tensor(zg[:, t, :], zs[:, t, :], gb_bc[:].rearrange("p (o d) -> p o d", o=1).broadcast_to([P, 2, D]),
                                ALU.mult).then_inc(s["zg_ready"], 1)
                wait(pool, "zg_ready", b * 2 + n + 1, "passed_pool")
                wait(pool, "res_stored", b * 16, "passed_pool")
                q.tensor_tensor(res[:, t, :], zg[:, t, :], x1[:, t, :], ALU.add).then_inc(s["res_ready"], 1)

            def mask(b, h):
                wait(pool, "exp_done", b * 48 + 3 * h + 1, "passed_pool")
                d = prob[:, h % 8, 0:4 * P].rearrange("p (a t) -> p a t", a=4)
                q.affine_select(out=d, in_=d, compare_op=ALU.is_ge, fill=0.0, base=0, pattern=[[0, 4], [1, P]],
                                channel_multiplier=-1).then_inc(s["masked"], 1)

            def one(i):
                for t in range(SLOTS):
                    if live(i):
                        mask(i, t)
                    do(steps, POOL_AT, i, t)

            steps = dict(
                norm_a=lambda b: norm(b, xa, xn_a, ve_a, nm_a, rs_a, "lna_ready", "rsa_ready", "xna_ready", "ta_ready"),
                norm_c=lambda b: norm(b, x1, xn_c, ve_c, nm_c, rs_c, "lnc_ready", "rsc_ready", "xnc_ready", "t2_ready"),
                spread=spread, normalise=normalise, add_bias=add_bias, residual=residual, finish=finish)
            q.memset(kz[:], 0.0)
            q.memset(qs[:], 0.0).then_inc(s["set_ready"], 1)
            q.memset(neg_half[:], -0.5).then_inc(s["set_ready"], 1)
            pool.wait_ge(s["set_ready"], 2)
            steps["norm_a"](0)
            q.memset(va[:], 1.0)
            q.memset(mask_qk[:, 0:S - P], 0.0).then_inc(s["set_ready"], 1)
            pool.wait_ge(s["set_ready"], 3)
            iterations(pool, one)


_INS = ["L0_attn_x", "L0_attn_w_qkv", "L0_attn_b_qkv", "L0_attn_w_out", "L0_attn_b_out", "L0_ffn_gate_W",
        "L0_ffn_expert_W", "L0_ffn_out_W", "L0_c", "L0_wmod"]


def constants():
    at = np.arange(P)
    qk = np.where(at[None, :] > at[:, None], -1e30, 0.0).astype(np.float32)
    kaug = np.zeros((STACK - PARTS, 16, 512), np.float16)
    qaug = np.zeros((STACK - PARTS, 8, 512), np.float16)
    kaug[0] = np.arange(512) * (FS / QONE)
    qaug[0] = QONE
    for r in range(1, CONST - PARTS):
        kaug[r, :, 32 * r:32 * r + 32] = FS
        qaug[r, :, 0:32 * r] = -60000.0
    kaug[CONST - PARTS, 0::2] = FS
    kaug[CONST - PARTS + 1, 1::2] = FS
    return {"ident": np.eye(P, dtype=np.float32), "mask_qk": qk, "kaug": kaug, "qaug": qaug}


def kernel(**inputs):
    import concourse.bacc as bacc
    from concourse.bass_utils import run_bass_kernel_spmd

    nc = bacc.Bacc("TRN2", target_bir_lowering=False, num_devices=1)
    arrays = {name: np.ascontiguousarray(inputs[name]) for name in _INS}
    arrays.update(constants())
    args = [nc.dram_tensor(f"in_{name}", a.shape, mybir.dt.from_np(a.dtype), kind="ExternalInput").ap()
            for name, a in arrays.items()]
    shape = arrays["L0_attn_x"].shape
    out = nc.dram_tensor("out_0", shape, F32, kind="ExternalOutput").ap()
    build(nc, *args, out)
    r = run_bass_kernel_spmd(nc, [{f"in_{name}": a for name, a in arrays.items()}], core_ids=[0])
    return r.results[0]["out_0"]
```
